# Optimizing a Trainium2 kernel written in Bass

```python
import numpy as np
import jax
import jax.numpy as jnp

def _softmax(x, axis=-1):
    return jax.nn.softmax(x, axis=axis)

def _gelu(x):
    return jax.nn.gelu(x, approximate=True)

def _silu(x):
    return jax.nn.silu(x)

def _sigmoid(x):
    return jax.nn.sigmoid(x)

def _layernorm(x, axis=-1, eps=1e-05):
    m = jnp.mean(x, axis=axis, keepdims=True)
    v = jnp.var(x, axis=axis, keepdims=True)
    return (x - m) / jnp.sqrt(v + eps)

def _scatter_add(tgt, idx, src, axis=0):
    return tgt.at[idx].add(src)

def _segment_sum(src, seg, n):
    return jax.ops.segment_sum(src, seg, n)
kernel_name = 'mk_gnn_preln_d4_gnn_r8_570dd1'

def setup_inputs(seed: int=0):
    np.random.seed(seed)
    _w = jnp.asarray

    def _rec_inputs():
        import jax
        import jax.numpy as jnp
        _gk = jax.random.key(seed)
        x = -0.000202 + 1 * jax.random.normal(jax.random.fold_in(_gk, 1), (6250, 64), jnp.float32)
        _s = jax.random.randint(jax.random.fold_in(_gk, 2), (100000,), 0, 6250, jnp.int32)
        _d = jax.random.randint(jax.random.fold_in(_gk, 3), (100000,), 0, 6250, jnp.int32)
        _loop = jnp.arange(6250, dtype=jnp.int32)
        src = jnp.concatenate([_s, _d, _loop])
        dst = jnp.concatenate([_d, _s, _loop])
        _o = jnp.argsort(dst, stable=True)
        src = src[_o]
        dst = dst[_o]
        edge_attr_32 = -5.3897e-05 + 0.999841 * jax.random.normal(jax.random.fold_in(_gk, 12), (206250, 32), jnp.float32)
        edge_attr_64 = -8.16379e-05 + 0.999858 * jax.random.normal(jax.random.fold_in(_gk, 13), (206250, 64), jnp.float32)
        return (x, src, dst, edge_attr_32, edge_attr_64)
    x, src, dst, edge_attr_32, edge_attr_64 = _rec_inputs()

    def _L0_gnn_setup():
        import jax, jax.numpy as jnp
        import numpy as np
        N = 12500
        E = 200000
        D = 64
        key = jax.random.key(seed)
        k1, k2, k3 = jax.random.split(key, 3)
        feat = jax.random.normal(k1, (N, D), dtype=jnp.float32)
        src = jax.random.randint(k2, (E,), 0, N, dtype=jnp.int32)
        dst = jax.random.randint(k3, (E,), 0, N, dtype=jnp.int32)
        beta = jnp.ones((1,), dtype=jnp.float32)
        return {'feat': feat, 'src': src, 'dst': dst, 'beta': beta}
    _L0_gnn_all = _L0_gnn_setup()
    _L0_gnn_in = {k: v for k, v in _L0_gnn_all.items() if k in ('beta',)}
    del _L0_gnn_all

    def _L1_gnn_setup():
        import jax, jax.numpy as jnp
        import numpy as np
        BN_EPS = 1e-05

        def _batchnorm(x, gamma, beta):
            m = jnp.mean(x, axis=0)
            v = jnp.var(x, axis=0)
            return (x - m) * jax.lax.rsqrt(v + BN_EPS) * gamma + beta
        N, E, D = (12500, 200000, 64)
        key = jax.random.key(seed)
        ks = jax.random.split(key, 6)
        return {'node_feats': jax.random.normal(ks[0], (N, D), dtype=jnp.float32), 'edge_feats': jax.random.normal(ks[1], (E, D), dtype=jnp.float32), 'src': jax.random.randint(ks[2], (E,), 0, N, dtype=jnp.int32), 'dst': jax.random.randint(ks[3], (E,), 0, N, dtype=jnp.int32), 'eps': jnp.zeros((1,), dtype=jnp.float32), 'W1': jax.random.normal(ks[4], (D, 2 * D), dtype=jnp.float32) * (1.0 / np.sqrt(D)), 'b1': jnp.zeros((2 * D,), dtype=jnp.float32), 'gamma1': jnp.ones((2 * D,), dtype=jnp.float32), 'beta1': jnp.zeros((2 * D,), dtype=jnp.float32), 'W2': jax.random.normal(ks[5], (2 * D, D), dtype=jnp.float32) * (1.0 / np.sqrt(2 * D)), 'b2': jnp.zeros((D,), dtype=jnp.float32), 'gamma2': jnp.ones((D,), dtype=jnp.float32), 'beta2': jnp.zeros((D,), dtype=jnp.float32)}
    _L1_gnn_all = _L1_gnn_setup()
    _L1_gnn_in = {k: v for k, v in _L1_gnn_all.items() if k in ('eps', 'W1', 'b1', 'gamma1', 'beta1', 'W2', 'b2', 'gamma2', 'beta2')}
    del _L1_gnn_all

    def _L2_gnn_setup():
        import jax, jax.numpy as jnp
        import numpy as np
        N_NODES = 6250
        N_EDGES = 100000
        D_NODE = 64
        D_EDGE = 32
        D_OUT = 64
        key = jax.random.key(seed)
        ks = jax.random.split(key, 8)
        node_feats = jax.random.normal(ks[0], (N_NODES, D_NODE), dtype=jnp.float32)
        edge_feats = jax.random.normal(ks[1], (N_EDGES, D_EDGE), dtype=jnp.float32)
        src = jax.random.randint(ks[2], (N_EDGES,), 0, N_NODES, dtype=jnp.int32)
        dst = jax.random.randint(ks[3], (N_EDGES,), 0, N_NODES, dtype=jnp.int32)
        d_in_e = D_NODE + D_EDGE + D_NODE
        d_in_v = D_OUT + D_NODE
        W_e = jax.random.normal(ks[4], (d_in_e, D_OUT), dtype=jnp.float32) / np.sqrt(d_in_e)
        b_e = jnp.zeros((D_OUT,), dtype=jnp.float32)
        W_v = jax.random.normal(ks[5], (d_in_v, D_OUT), dtype=jnp.float32) / np.sqrt(d_in_v)
        b_v = jnp.zeros((D_OUT,), dtype=jnp.float32)
        return {'node_feats': node_feats, 'edge_feats': edge_feats, 'src': src, 'dst': dst, 'W_e': W_e, 'b_e': b_e, 'W_v': W_v, 'b_v': b_v}
    _L2_gnn_all = _L2_gnn_setup()
    _L2_gnn_in = {k: v for k, v in _L2_gnn_all.items() if k in ('W_e', 'b_e', 'W_v', 'b_v')}
    del _L2_gnn_all

    def _L3_gnn_setup():
        import jax, jax.numpy as jnp
        import numpy as np
        key = jax.random.key(seed)
        k1, k2 = jax.random.split(key)
        N, D, E = (12500, 64, 200000)
        x = jax.random.normal(k1, (N, D), dtype=jnp.float32)
        edge_index = jax.random.randint(k2, (2, E), 0, N, dtype=jnp.int64)
        return {'x': x, 'edge_index': edge_index}
    _L3_gnn_all = _L3_gnn_setup()
    _L3_gnn_in = {k: v for k, v in _L3_gnn_all.items() if k in ()}
    del _L3_gnn_all
    return {'x': x, 'src': src, 'dst': dst, 'edge_attr_32': edge_attr_32, 'edge_attr_64': edge_attr_64, 'L0_gnn_beta': _L0_gnn_in['beta'], 'L1_gnn_eps': _L1_gnn_in['eps'], 'L1_gnn_W1': _L1_gnn_in['W1'], 'L1_gnn_b1': _L1_gnn_in['b1'], 'L1_gnn_gamma1': _L1_gnn_in['gamma1'], 'L1_gnn_beta1': _L1_gnn_in['beta1'], 'L1_gnn_W2': _L1_gnn_in['W2'], 'L1_gnn_b2': _L1_gnn_in['b2'], 'L1_gnn_gamma2': _L1_gnn_in['gamma2'], 'L1_gnn_beta2': _L1_gnn_in['beta2'], 'L2_gnn_W_e': _L2_gnn_in['W_e'], 'L2_gnn_b_e': _L2_gnn_in['b_e'], 'L2_gnn_W_v': _L2_gnn_in['W_v'], 'L2_gnn_b_v': _L2_gnn_in['b_v']}

def reference(x, src, dst, edge_attr_32, edge_attr_64, L0_gnn_beta, L1_gnn_eps, L1_gnn_W1, L1_gnn_b1, L1_gnn_gamma1, L1_gnn_beta1, L1_gnn_W2, L1_gnn_b2, L1_gnn_gamma2, L1_gnn_beta2, L2_gnn_W_e, L2_gnn_b_e, L2_gnn_W_v, L2_gnn_b_v):
    import jax
    import jax.numpy as jnp

    def _L0_gnn_ref(feat, src, dst, beta):
        import jax, jax.numpy as jnp
        import numpy as np
        N = 12500
        E = 200000
        D = 64
        n = feat.shape[0]
        nrm = jnp.sqrt(jnp.sum(feat * feat, axis=-1, keepdims=True))
        norm_h = feat / jnp.maximum(nrm, 1e-12)
        cos = jnp.sum(norm_h[src] * norm_h[dst], axis=-1)
        e = beta[0] * cos
        emax = jax.ops.segment_max(e, dst, num_segments=n)
        emax = jnp.where(jnp.isfinite(emax), emax, 0.0)
        p = jnp.exp(e - emax[dst])
        psum = jax.ops.segment_sum(p, dst, num_segments=n)
        p = p / jnp.maximum(psum, 1e-38)[dst]
        out = jax.ops.segment_sum(feat[src] * p[:, None], dst, num_segments=n)
        return out

    def _L1_gnn_ref(node_feats, edge_feats, src, dst, eps, W1, b1, gamma1, beta1, W2, b2, gamma2, beta2):
        import jax, jax.numpy as jnp
        import numpy as np
        BN_EPS = 1e-05

        def _batchnorm(x, gamma, beta):
            m = jnp.mean(x, axis=0)
            v = jnp.var(x, axis=0)
            return (x - m) * jax.lax.rsqrt(v + BN_EPS) * gamma + beta
        N = node_feats.shape[0]
        msg = node_feats[src] + edge_feats
        agg_sum = jax.ops.segment_sum(msg, dst, num_segments=N)
        deg = jax.ops.segment_sum(jnp.ones((src.shape[0],), dtype=node_feats.dtype), dst, num_segments=N)
        agg_mean = agg_sum / jnp.maximum(deg, 1.0)[:, None]
        h = (1.0 + eps[0]) * node_feats + agg_mean
        h = jax.nn.relu(_batchnorm(h @ W1 + b1, gamma1, beta1))
        h = jax.nn.relu(_batchnorm(h @ W2 + b2, gamma2, beta2))
        return h

    def _L2_gnn_ref(node_feats, edge_feats, src, dst, W_e, b_e, W_v, b_v):
        import jax, jax.numpy as jnp
        import numpy as np
        N_NODES = 6250
        N_EDGES = 100000
        D_NODE = 64
        D_EDGE = 32
        D_OUT = 64
        n_nodes = node_feats.shape[0]
        x_e = jnp.concatenate([node_feats[src], edge_feats, node_feats[dst]], axis=1)
        m = jax.nn.relu(x_e @ W_e + b_e)
        msum = jax.ops.segment_sum(m, dst, num_segments=n_nodes)
        deg = jax.ops.segment_sum(jnp.ones((dst.shape[0],), dtype=m.dtype), dst, num_segments=n_nodes)
        neigh = jnp.where(deg[:, None] > 0, msum / jnp.maximum(deg[:, None], 1.0), 0.0)
        x_v = jnp.concatenate([neigh, node_feats], axis=1)
        return jax.nn.relu(x_v @ W_v + b_v)

    def _L3_gnn_ref(x, edge_index):
        import jax, jax.numpy as jnp
        import numpy as np
        src = edge_index[0]
        dst = edge_index[1]
        msgs = x[src]
        out = jax.ops.segment_sum(msgs, dst, num_segments=x.shape[0])
        return out
    edge_index = jnp.stack([src, dst])
    h = jnp.maximum(_layernorm(x, axis=-1), 0.0)
    x = x + _L0_gnn_ref(h, src, dst, L0_gnn_beta)
    h = jnp.maximum(_layernorm(x, axis=-1), 0.0)
    x = x + _L1_gnn_ref(h, edge_attr_64, src, dst, L1_gnn_eps, L1_gnn_W1, L1_gnn_b1, L1_gnn_gamma1, L1_gnn_beta1, L1_gnn_W2, L1_gnn_b2, L1_gnn_gamma2, L1_gnn_beta2)
    h = jnp.maximum(_layernorm(x, axis=-1), 0.0)
    x = x + _L2_gnn_ref(h, edge_attr_32, src, dst, L2_gnn_W_e, L2_gnn_b_e, L2_gnn_W_v, L2_gnn_b_v)
    h = jnp.maximum(_layernorm(x, axis=-1), 0.0)
    x = x + _L3_gnn_ref(h, edge_index)
    return x

_drawn_inputs = setup_inputs


def setup_inputs(seed=0):
    import zlib

    import numpy as np

    out = dict(_drawn_inputs(seed))
    spreads = {'L1_gnn_b1': (0.0, 0.8),
     'L1_gnn_gamma1': (1.0, 0.2),
     'L1_gnn_beta1': (0.0, 0.469),
     'L1_gnn_b2': (0.0, 0.8),
     'L1_gnn_gamma2': (1.0, 0.2),
     'L1_gnn_beta2': (0.0, 0.1),
     'L2_gnn_b_e': (0.0, 0.395),
     'L2_gnn_b_v': (0.0, 0.1)}
    factors = {'edge_attr_32': 8.0}
    for name, (base, spread) in spreads.items():
        noise = np.random.default_rng([zlib.crc32(name.encode()), seed]).standard_normal(out[name].shape)
        drawn = base * np.exp(spread * noise) if base else spread * noise
        out[name] = jnp.asarray(drawn.astype(out[name].dtype))
    for name, factor in factors.items():
        out[name] = (out[name] * factor).astype(out[name].dtype)
    return out
```

```python
import numpy as np
import concourse.bass as bass
from concourse import mybir
from contextlib import ExitStack

F32 = mybir.dt.float32
I32 = mybir.dt.int32
I16 = mybir.dt.int16
ALU = mybir.AluOpType
ACT = mybir.ActivationFunctionType
AX = mybir.AxisListType

N, E, D = 6250, 206250, 64
D_EDGE = 32
P = 128
NT = -(-N // P)
NPAD = P * NT
NROWS = NPAD + P
G = 13
T = -(-E // P)
C = T // G
EC = G * P
W = 64
NO_NODE = 16384
MAX_PASSES = N // W + 1
BIG = 1.0e30
LN_EPS = BN_EPS = 1e-5
ROW0 = D + 2
ST0 = 2 * D + 3
S_DEN, S_MAX, S_EA, S_DEG = D, D + 1, D + 2, 2 * D + 2
NQ = -(-NPAD // 512)
assert T == C * G and C % 2 == 0 and N + W <= NROWS


def gnn_layers(nc, x_in, src_c, dst_c, dst_r, ea32_t, ea64_c, beta, eps, w1, b1, gamma1, beta1,
               w2, b2, gamma2, beta2, w_e, b_e, w_v, b_v, out):
    ctx = ExitStack()
    with ctx:
        def sb(name, shape, dt=F32):
            return ctx.enter_context(nc.sbuf_tensor(name, shape, dt))

        def ps(name, shape):
            return ctx.enter_context(nc.psum_tensor(name, shape, F32))

        def sem(name):
            return ctx.enter_context(nc.semaphore(name))

        def dram(name, shape, dt=F32):
            return nc.dram_tensor(name, shape, dt, kind="Internal").ap()

        h0_rows = dram("h0_rows", (NPAD, ROW0))
        h_rows = [dram(f"h_rows{i}", (NPAD, D)) for i in range(3)]
        win_rows = [dram(f"win_rows{i}", (NROWS, D)) for i in range(2)]
        state0 = dram("state0", (NROWS, ST0))
        sums = [dram(f"sums{i}", (NROWS, D)) for i in range(3)]
        span_d = dram("span_d", (C, 2))
        rel_rows = dram("rel_rows", (C, EC), I16)

        x = sb("x", [P, NT, D])
        h = sb("h", [P, NT, D])
        tmp = sb("tmp", [P, NT, D])
        arena = sb("arena", [P, NT * ST0])
        state = arena[:, :].rearrange("p (t f) -> p t f", f=ST0)
        cat = arena[:, 0:NT * 2 * D].rearrange("p (t f) -> p t f", f=2 * D)
        y1t = arena[:, 0:NPAD]
        hT = sb("hT", [P, NPAD])
        ident = sb("ident", [P, P])
        ones = sb("ones", [P, P])
        col = sb("col", [P, 8, NT])
        w1_sb = sb("w1_sb", [D, 2 * D])
        w2_sb = sb("w2_sb", [2 * D, D])
        wsd_sb = sb("wsd_sb", [D + 1, 2 * D])
        wv_sb = sb("wv_sb", [2 * D, D])
        bv_sb = sb("bv_sb", [P, D])
        par = sb("par", [P, 8])
        bn1 = sb("bn1", [P, NQ, 6])
        bna = sb("bna", [P, 8])
        src_sb = sb("src_sb", [P, T], I32)
        dcol = sb("dcol", [P, T])
        iota_row = sb("iota_row", [P, 2, W])
        iota_col = sb("iota_col", [P, 2])
        base0 = sb("base0", [1, C], I32)
        base = sb("base", [1, C], I32)
        spans = sb("spans", [P, C, 2])
        stat = sb("stat", [P, 8])
        passes = sb("passes", [1, 2], I32)
        idx = sb("idx", [P, 2, G], I32)
        g = sb("g", [P, 2, G, ROW0])
        onehot = sb("onehot", [P, G, W])
        weighted = sb("weighted", [P, G, W])
        lhs = sb("lhs", [W + D_EDGE, 2, EC])
        off_window = sb("off_window", [W, EC])
        drow = sb("drow", [W, 2, EC], I16)
        ea = sb("ea", [P, 2, G, D + 1])
        win = sb("win", [W + D_EDGE, 2, D])
        sc = sb("sc", [P, 4, G])
        st_in = sb("st_in", [W, ST0])
        st_out = sb("st_out", [W, ST0])
        mrg = sb("mrg", [W, 8])
        rel16 = weighted[:, :, :].rearrange("p g w -> p (g w)").bitcast(I16)[:, 0:EC]
        ps_x = ps("ps_x", [P, 16, W])
        ps_t = ps("ps_t", [P, 16, P])
        ps_a = ps("ps_a", [P, 512])
        ps_b = ps("ps_b", [P, 512])
        banks = [ps_t[:, 4 * i:4 * i + 4, :].rearrange("p a b -> p (a b)") for i in range(4)]

        def iota_rows():
            return iota_row[:, 1, :].rearrange("p (o w) -> p o w", o=1).to_broadcast([P, G, W])

        def per_edge(a):
            return a.rearrange("p (g o) -> p g o", o=1).to_broadcast([P, G, W])

        def per_node(a):
            return a.rearrange("p (t o) -> p t o", o=1).to_broadcast([P, NT, D])

        def node_rows(table, width):
            return table[0:NPAD, 0:width].rearrange("(p t) f -> p t f", t=NT)

        s_load = sem("s_load")
        s_vec = sem("s_vec")
        s_act = sem("s_act")
        s_pool = sem("s_pool")
        s_pe = sem("s_pe")
        s_store = sem("s_store")
        s_spans = sem("s_spans")
        d_step = sem("d_step")
        counts = {}

        def bump(which, ins, by=1):
            ins.then_inc(which, by)
            counts[which.name] = counts.get(which.name, 0) + by
            return counts.get(which.name, 0)

        def at(which):
            return counts.get(which.name, 0)

        def link(eng, ins):
            eng.wait_ge(s_vec, bump(s_vec, ins))

        with nc.Block() as block:
            @block.sync
            def _(sp):
                def load(dst, src):
                    bump(s_load, sp.dma_start(dst, src), 16)

                load(x[:, :, :], x_in.rearrange("(p t) f -> p t f", t=NT))
                load(src_sb[:, :], src_c)
                load(arena[:, 0:T].bitcast(I32), dst_c)
                load(hT[0:C, 0:EC].bitcast(I32), dst_r)
                with nc.allow_non_contiguous_dma("a value per partition"):
                    load(par[:, 0:1], b1.rearrange("(p o) -> p o", o=1))
                    load(par[:, 1:2], gamma1.rearrange("(p o) -> p o", o=1))
                    load(par[:, 2:3], beta1.rearrange("(p o) -> p o", o=1))
                    load(par[0:D, 3:4], b2.rearrange("(p o) -> p o", o=1))
                    load(par[0:D, 4:5], gamma2.rearrange("(p o) -> p o", o=1))
                    load(par[0:D, 5:6], beta2.rearrange("(p o) -> p o", o=1))
                    load(par[:, 6:7], beta.rearrange("(p o) -> p o", o=1).to_broadcast([P, 1]))
                    load(par[:, 7:8], eps.rearrange("(p o) -> p o", o=1).to_broadcast([P, 1]))
                load(w1_sb[:, :], w1)
                load(w2_sb[:, :], w2)
                load(wsd_sb[0:D, 0:D], w_e[0:D, :])
                load(wsd_sb[0:D, D:2 * D], w_e[D + D_EDGE:2 * D + D_EDGE, :])
                load(wsd_sb[D:D + 1, D:2 * D], b_e.rearrange("(o f) -> o f", o=1))
                for j in range(2):
                    load(win[W:W + D_EDGE, j, :], w_e[D:D + D_EDGE, :])
                load(wv_sb[:, :], w_v)
                load(bv_sb[:, :], b_v.rearrange("(o f) -> o f", o=1).to_broadcast([P, D]))

            @block.gpsimd
            def _(pool):
                pool.memset(ident[:, :], 0.0).then_inc(s_pool, 1)
                pool.wait_ge(s_pool, 1)
                pool.affine_select(out=ident[:, :], in_=ident[:, :], compare_op=ALU.not_equal, fill=1.0,
                                   base=0, pattern=[[-1, P]], channel_multiplier=1).then_inc(s_pool, 1)
                pool.iota(iota_row[:, 0, :], pattern=[[1, W]], base=0, channel_multiplier=0,
                          allow_small_or_imprecise_dtypes=True).then_inc(s_pool, 1)
                pool.iota(iota_col[:, 0:1], pattern=[[0, 1]], base=0, channel_multiplier=1,
                          allow_small_or_imprecise_dtypes=True).then_inc(s_pool, 1)
                pool.wait_ge(s_pool, 4)

            @block.vector
            def _(dve):
                dve.memset(ea[:, :, :, D:D + 1], 1.0)
                dve.memset(wsd_sb[D:D + 1, 0:D], 0.0)
                link(dve, dve.memset(tmp[:, :, :], 0.0))
                dve.wait_ge(s_load, at(s_load))

        with nc.Block() as block:
            @block.vector
            def _(dve):
                dst, dstf, real = hT[0:C, 0:EC].bitcast(I32), hT[0:C, 2048:2048 + EC], hT[0:C, 4096:4096 + EC]
                link(dve, dve.tensor_copy(dstf, dst))
                link(dve, dve.tensor_reduce(stat[0:C, 0:1], dstf, AX.X, ALU.min))
                link(dve, dve.tensor_scalar(real, dstf, float(N), None, ALU.is_lt))
                link(dve, dve.tensor_tensor(real, dstf, real, ALU.mult))
                link(dve, dve.tensor_reduce(stat[0:C, 2:3], real, AX.X, ALU.max))
                link(dve, dve.tensor_tensor(stat[0:C, 1:2], stat[0:C, 2:3], stat[0:C, 0:1], ALU.subtract))
                counts["spans known"] = at(s_vec)
                link(dve, dve.tensor_scalar(rel16[0:C, :], dstf, stat[0:C, 0:1], None, ALU.subtract))
                counts["rows relative"] = at(s_vec)
                dve.wait_ge(s_spans, 16)
                link(dve, dve.tensor_copy(base0[0:1, :], spans[0:1, :, 0]))
                link(dve, dve.tensor_reduce(stat[0:1, 4:5], spans[0:1, :, 1], AX.X, ALU.max))
                link(dve, dve.tensor_copy(passes[0:1, 0:1], stat[0:1, 4:5]))
                link(dve, dve.tensor_scalar(passes[0:1, 0:1], passes[0:1, 0:1], W.bit_length() - 1, None,
                                            ALU.arith_shift_right))
                link(dve, dve.tensor_scalar(passes[0:1, 1:2], passes[0:1, 0:1], 1.0, None, ALU.add))
                link(dve, dve.tensor_copy(dcol[:, :], arena[:, 0:T].bitcast(I32)))
                link(dve, dve.tensor_tensor(
                    dcol[:, :].rearrange("p (c g) -> p c g", g=G),
                    dcol[:, :].rearrange("p (c g) -> p c g", g=G),
                    spans[:, :, 0:1].to_broadcast([P, C, G]), ALU.subtract))

            @block.sync
            def _(sp):
                sp.wait_ge(s_vec, counts["spans known"])
                sp.dma_start(span_d, stat[0:C, 0:2]).then_inc(s_store, 16)
                sp.wait_ge(s_store, 16)
                sp.dma_start(spans[:, :, :], span_d.rearrange("(o c) f -> o c f", o=1)
                             .to_broadcast([P, C, 2])).then_inc(s_spans, 16)
                sp.wait_ge(s_vec, counts["rows relative"])
                sp.dma_start(rel_rows, rel16[0:C, :]).then_inc(s_store, 16)
                sp.wait_ge(s_store, 32)
                counts[s_store.name] = 32

        with nc.Block() as block:
            @block.vector
            def _(dve):
                link(dve, dve.memset(arena[:, :], 0.0))
                link(dve, dve.memset(state[:, :, S_MAX:S_MAX + 1], -BIG))
                counts["zeroed"] = at(s_vec)

            @block.sync
            def _(sp):
                sp.wait_ge(s_vec, counts["zeroed"])
                bump(s_store, sp.dma_start(node_rows(state0, ST0), state), 16)
                bump(s_store, sp.dma_start(state0[NPAD:NROWS, :], state[:, 0, :]), 16)
                for table in sums + win_rows:
                    bump(s_store, sp.dma_start(node_rows(table, D), tmp[:, :, :]), 16)
                    bump(s_store, sp.dma_start(table[NPAD:NROWS, :], tmp[:, 0, :]), 16)
                sp.wait_ge(s_store, at(s_store))

        def layernorm_relu():
            mean, var = col[:, 0, :], col[:, 1, :]
            with nc.Block() as block:
                @block.vector
                def _(dve):
                    link(dve, dve.tensor_reduce(mean, x[:, :, :], AX.X, ALU.add))
                    link(dve, dve.tensor_scalar(mean, mean, 1.0 / D, None, ALU.mult))
                    link(dve, dve.tensor_tensor(h[:, :, :], x[:, :, :], per_node(mean), ALU.subtract))
                    link(dve, dve.tensor_tensor(tmp[:, :, :], h[:, :, :], h[:, :, :], ALU.mult))
                    link(dve, dve.tensor_reduce(var, tmp[:, :, :], AX.X, ALU.add))
                    link(dve, dve.tensor_scalar(var, var, 1.0 / D, LN_EPS, ALU.mult, ALU.add))
                    counts["variance"] = at(s_vec)
                    dve.wait_ge(s_act, at(s_act) + 1)
                    link(dve, dve.reciprocal(var, var))
                    link(dve, dve.tensor_tensor(h[:, :, :], h[:, :, :], per_node(var), ALU.mult))
                    link(dve, dve.tensor_scalar(h[:, :, :], h[:, :, :], 0.0, None, ALU.max))

                @block.scalar
                def _(act):
                    act.wait_ge(s_vec, counts["variance"])
                    bump(s_act, act.activation(var, var, ACT.Sqrt))

        def transpose_nodes(rows, width, to):
            first, done = at(s_pe), at(s_vec)
            by_node = to.rearrange("f (p t) -> f t p", t=NT)
            starts = list(range(0, NT, 4))
            with nc.Block() as block:
                @block.tensor
                def _(pe):
                    for n, t0 in enumerate(starts):
                        if n >= 2:
                            pe.wait_ge(s_vec, done + n - 1)
                        for t in range(t0, min(t0 + 4, NT)):
                            last = pe.transpose(banks[n % 2][0:width, (t - t0) * P:(t - t0 + 1) * P],
                                                rows[:, t, :], ident[:, :])
                        bump(s_pe, last)

                @block.vector
                def _(dve):
                    for n, t0 in enumerate(starts):
                        dve.wait_ge(s_pe, first + n + 1)
                        k = min(4, NT - t0)
                        bump(s_vec, dve.tensor_copy(
                            by_node[:, t0:t0 + k, :],
                            banks[n % 2][0:width, 0:k * P].rearrange("f (t p) -> f t p", t=k)))
                    dve.wait_ge(s_vec, at(s_vec))

        def project(weights, rows_in, to, bias, gamma, shift, width, stats):
            pe0, act0 = at(s_pe), at(s_act)
            mv, scale = bna[0:width, 0:2], bna[0:width, 2:3]
            with nc.Block() as block:
                @block.tensor
                def _(pe):
                    for q in range(NQ):
                        n = min(512, NPAD - 512 * q)
                        if q >= 2:
                            pe.wait_ge(s_act, act0 + q - 1)
                        bump(s_pe, pe.matmul(banks[q % 2][0:width, 0:n], weights,
                                             rows_in[:, 512 * q:512 * q + n], start=True, stop=True))

                @block.scalar
                def _(act):
                    for q in range(NQ):
                        n = min(512, NPAD - 512 * q)
                        act.wait_ge(s_pe, pe0 + q + 1)
                        bump(s_act, act.activation(to[:, 512 * q:512 * q + n], banks[q % 2][0:width, 0:n],
                                                   ACT.Identity, bias=bias))

                @block.vector
                def _(dve):
                    for q in range(NQ):
                        n = min(512, N - 512 * q)
                        dve.wait_ge(s_act, act0 + q + 1)
                        link(dve, dve.bn_stats(stats[0:width, q, :], to[:, 512 * q:512 * q + n]))
                    link(dve, dve.bn_aggr(mv, stats[0:width, :, :].rearrange("p q s -> p (q s)")))
                    link(dve, dve.tensor_scalar(scale, mv[:, 1:2], BN_EPS, None, ALU.add))
                    counts["variance"] = at(s_vec)

            with nc.Block() as block:
                @block.vector
                def _(dve):
                    dve.wait_ge(s_act, at(s_act) + 1)
                    link(dve, dve.reciprocal(scale, scale))
                    link(dve, dve.tensor_tensor(scale, scale, gamma, ALU.mult))
                    link(dve, dve.tensor_tensor(bna[0:width, 3:4], mv[:, 0:1], scale, ALU.mult))
                    link(dve, dve.tensor_tensor(bna[0:width, 4:5], shift, bna[0:width, 3:4], ALU.subtract))
                    counts["affine"] = at(s_vec)

                @block.scalar
                def _(act):
                    bump(s_act, act.activation(scale, scale, ACT.Sqrt))
                    act.wait_ge(s_vec, counts["affine"])
                    bump(s_act, act.activation(to, to, ACT.Relu, scale=scale, bias=bna[0:width, 4:5]))
                    act.wait_ge(s_act, at(s_act))

        def store_rows(pairs):
            with nc.Block() as block:
                @block.sync
                def _(sp):
                    for table, rows in pairs:
                        bump(s_store, sp.dma_start(table, rows), 16)
                    sp.wait_ge(s_store, at(s_store))

        def load_rows(rows, table):
            with nc.Block() as block:
                @block.sync
                def _(sp):
                    bump(s_load, sp.dma_start(rows, table), 16)
                    sp.wait_ge(s_load, at(s_load))

        e = {name: sem("e_" + name) for name in (
            "idx", "gathering", "reducing", "loading", "rows0", "rows1", "rel0", "rel1", "attr0", "attr1", "win0", "win1", "hot", "dst",
            "score", "spread", "top", "topped", "lowered", "p", "weighted", "summed", "attr_summed",
            "state", "pair", "scales", "merged", "stored")}
        START = {"hot": 2, "dst": 2, "summed": 2, "attr_summed": 2,
                 "lowered": 1, "merged": 1, "top": 1, "score": 1}

        def done(name, k):
            return k + 1 + START.get(name, 0)

        def start_counts(eng, *names):
            for name in names:
                eng.sem_inc(e[name], START[name])

        def start_windows():
            with nc.Block() as block:
                @block.vector
                def _(dve):
                    bump(s_vec, dve.tensor_copy(base[:, :], base0[:, :]))
                    bump(s_vec, dve.tensor_copy(iota_row[:, 1, :], iota_row[:, 0, :]))
                    link(dve, dve.tensor_copy(iota_col[:, 1:2], iota_col[:, 0:1]))

        def next_windows():
            with nc.Block() as block:
                @block.vector
                def _(dve):
                    dve.tensor_scalar(base[:, :], base[:, :], float(W), float(N), ALU.add, ALU.min)
                    dve.tensor_scalar(iota_row[:, 1, :], iota_row[:, 1, :], float(W), None, ALU.add)
                    dve.tensor_scalar(iota_col[:, 1:2], iota_col[:, 1:2], float(W), None, ALU.add)

        def over_windows(one_pass):
            start_windows()
            n = nc.values_load(passes[0:1, 1:2], min_val=1, max_val=MAX_PASSES)
            with nc.Fori(0, n):
                nc.gpsimd.dma_reset()
                nc.all_engine_barrier()
                for s in [*e.values(), d_step]:
                    nc.sync.sem_clear(s)
                nc.all_engine_barrier()
                one_pass()
                next_windows()

        def chunks(eng):
            return eng.Fori(0, C // 2)

        def gather_chunks(pool, table, width):
            with pool.Fori(0, C // 2) as i:
                for j in range(2):
                    k = i * 2 + j
                    pool.wait_ge(e["summed"], done("summed", k - 2))
                    pool.tensor_copy(idx[:, j, :], src_sb[:, bass.ds(k * G, G)]).then_inc(e["idx"], 1)
                    pool.wait_ge(e["idx"], k + 1)
                    pool.sem_inc(e["gathering"], 1)
                    for t in range(G):
                        pool.indirect_dma_start(
                            g[:, j, t, 0:width], None, table,
                            bass.IndirectOffsetOnAxis(ap=idx[:, j, t:t + 1], axis=0)
                        ).then_inc(e[f"rows{j}"], 16)
            for j in range(2):
                pool.wait_ge(e[f"rows{j}"], C // 2 * G * 16)

        def window_of(eng, k):
            return eng.value_load(base[0:1, bass.ds(k, 1)], min_val=0, max_val=N)

        def attention_pass():
            with nc.Block() as block:
                @block.gpsimd
                def _(pool):
                    gather_chunks(pool, h0_rows, ROW0)

                @block.sync
                def _(sp):
                    with sp.Fori(0, C // 2) as i:
                        for j in range(2):
                            k = i * 2 + j
                            window = window_of(sp, k)
                            sp.wait_ge(e["hot"], done("hot", k - 2))
                            sp.sem_inc(e["loading"], 1)
                            sp.dma_start(drow[:, j, :], rel_rows[bass.ds(k, 1), :]
                                         .to_broadcast([W, EC])).then_inc(e[f"rel{j}"], 16)
                            sp.wait_ge(e["attr_summed"], done("attr_summed", k - 2))
                            sp.sem_inc(e["loading"], 1)
                            sp.dma_start(ea[:, j, :, 0:D], ea64_c[bass.ds(k, 1), :, :, :]
                                         .rearrange("o p g f -> (o p) g f")).then_inc(e[f"attr{j}"], 16)
                            sp.wait_ge(e["dst"], done("dst", k - 2))
                            sp.sem_inc(e["loading"], 1)
                            sp.dma_start(win[0:W, j, :], win_rows[0][bass.ds(window, W), :]
                                         ).then_inc(e[f"win{j}"], 16)

                @block.tensor
                def _(pe):
                    start_counts(pe, "dst", "summed", "attr_summed")
                    with pe.Fori(0, C // 2) as i:
                        for j in range(2):
                            k = i * 2 + j
                            pe.wait_ge(e["hot"], done("hot", k))
                            pe.wait_ge(e[f"win{j}"], i * 16 + 16)
                            pe.wait_ge(e["lowered"], done("lowered", k - 1))
                            for t in range(G):
                                last = pe.matmul(ps_x[:, t, :], lhs[0:W, j, t * P:(t + 1) * P],
                                                 win[0:W, j, :], start=True, stop=True)
                            last.then_inc(e["dst"], 1)
                            pe.wait_ge(e[f"attr{j}"], i * 16 + 16)
                            pe.wait_ge(e["merged"], done("merged", k - 1))
                            for t in range(G):
                                last = pe.matmul(ps_b[0:W, 0:D + 1], onehot[:, t, :], ea[:, j, t, :],
                                                 start=(t == 0), stop=(t == G - 1))
                            last.then_inc(e["attr_summed"], 1)
                            pe.wait_ge(e["score"], done("score", k))
                            pe.wait_ge(e["top"], done("top", k - 1))
                            for t in range(G):
                                last = pe.matmul(ps_t[0:W, t, :], sc[:, 0, t:t + 1].to_broadcast([P, W]),
                                                 ident[:, :], start=True, stop=True)
                            last.then_inc(e["spread"], 1)
                            pe.wait_ge(e["top"], done("top", k))
                            for t in range(G):
                                last = pe.matmul(ps_x[:, G, t:t + 1], lhs[0:W, j, t * P:(t + 1) * P],
                                                 mrg[:, 0:1], start=True, stop=True)
                            last.then_inc(e["topped"], 1)
                            pe.wait_ge(e["weighted"], k + 1)
                            for t in range(G):
                                last = pe.matmul(ps_a[0:W, 0:D + 1], weighted[:, t, :], g[:, j, t, 0:D + 1],
                                                 start=(t == 0), stop=(t == G - 1))
                            last.then_inc(e["summed"], 1)

                @block.vector
                def _(dve):
                    start_counts(dve, "hot", "lowered", "merged", "top", "score")
                    with dve.Fori(0, C // 2) as i:
                        for j in range(2):
                            k = i * 2 + j
                            dve.wait_ge(e["summed"], done("summed", k - 1))
                            dve.wait_ge(e["attr_summed"], done("attr_summed", k - 1))
                            dve.tensor_tensor(onehot[:, :, :], per_edge(dcol[:, bass.ds(k * G, G)]),
                                              iota_rows(), ALU.is_equal)
                            dve.wait_ge(e[f"rel{j}"], i * 16 + 16)
                            dve.tensor_scalar(off_window[:, :], drow[:, j, :], iota_col[0:W, 1:2], -BIG,
                                              ALU.not_equal, ALU.mult)
                            dve.tensor_scalar(lhs[0:W, j, :], drow[:, j, :], iota_col[0:W, 1:2], None,
                                              ALU.is_equal).then_inc(e["hot"], 1)
                            dve.wait_ge(e[f"rows{j}"], i * (16 * G) + 16 * G)
                            dve.wait_ge(e["dst"], done("dst", k))
                            dve.tensor_tensor(weighted[:, :, :], g[:, j, :, 0:D], ps_x[:, 0:G, :],
                                              ALU.mult).then_inc(d_step, 1)
                            dve.wait_ge(d_step, k * 4 + 1)
                            dve.tensor_reduce(sc[:, 1, :], weighted[:, :, :], AX.X, ALU.add
                                              ).then_inc(d_step, 1)
                            dve.wait_ge(d_step, k * 4 + 2)
                            dve.scalar_tensor_tensor(sc[:, 0, :], sc[:, 1, :], par[:, 6:7], g[:, j, :, D + 1],
                                                     ALU.mult, ALU.mult).then_inc(e["score"], 1)
                            dve.wait_ge(e["spread"], k + 1)
                            dve.sem_inc(e["reducing"], 1)
                            dve.tensor_tensor_reduce(
                                out=off_window[:, :].rearrange("w (g p) -> w g p", p=P),
                                in0=ps_t[0:W, 0:G, :],
                                in1=off_window[:, :].rearrange("w (g p) -> w g p", p=P),
                                scale=1.0, scalar=-BIG, op0=ALU.add, op1=ALU.max,
                                accum_out=mrg[:, 0:1]).then_inc(e["top"], 1)
                            dve.wait_ge(e["topped"], k + 1)
                            dve.tensor_tensor(sc[:, 2, :], sc[:, 0, :], ps_x[:, G, 0:G],
                                              ALU.subtract).then_inc(e["lowered"], 1)
                            dve.wait_ge(e["state"], k * 16 + 16)
                            dve.wait_ge(e["top"], done("top", k))
                            dve.tensor_tensor(mrg[:, 1:2], mrg[:, 0:1], st_in[:, S_MAX:S_MAX + 1],
                                              ALU.max).then_inc(d_step, 1)
                            dve.wait_ge(d_step, k * 4 + 3)
                            dve.tensor_tensor(mrg[:, 2:3], st_in[:, S_MAX:S_MAX + 1], mrg[:, 1:2],
                                              ALU.subtract)
                            dve.tensor_tensor(mrg[:, 3:4], mrg[:, 0:1], mrg[:, 1:2],
                                              ALU.subtract).then_inc(e["pair"], 1)
                            dve.wait_ge(e["p"], k + 1)
                            dve.tensor_tensor(weighted[:, :, :], onehot[:, :, :], per_edge(sc[:, 3, :]),
                                              ALU.mult).then_inc(e["weighted"], 1)
                            dve.wait_ge(e["scales"], k + 1)
                            dve.tensor_scalar(st_out[:, 0:D + 1], st_in[:, 0:D + 1], mrg[:, 4:5], None,
                                              ALU.mult).then_inc(d_step, 1)
                            dve.tensor_copy(st_out[:, S_MAX:S_MAX + 1], mrg[:, 1:2])
                            dve.tensor_tensor(st_out[:, S_EA:ST0], st_in[:, S_EA:ST0],
                                              ps_b[0:W, 0:D + 1], ALU.add)
                            dve.wait_ge(e["summed"], done("summed", k))
                            dve.wait_ge(d_step, k * 4 + 4)
                            dve.scalar_tensor_tensor(st_out[:, 0:D + 1], ps_a[0:W, 0:D + 1], mrg[:, 5:6],
                                                     st_out[:, 0:D + 1], ALU.mult, ALU.add
                                                     ).then_inc(e["merged"], 1)


                @block.scalar
                def _(act):
                    with act.Fori(0, C // 2) as i:
                        for j in range(2):
                            k = i * 2 + j
                            window = window_of(act, k)
                            rows = state0[bass.ds(window, W), :]
                            act.dma_start(st_in[:, :], rows).then_inc(e["state"], 16)
                            act.wait_ge(e["lowered"], done("lowered", k))
                            act.activation(sc[:, 3, :], sc[:, 2, :], ACT.Exp).then_inc(e["p"], 1)
                            act.wait_ge(e["pair"], k + 1)
                            act.activation(mrg[:, 4:6], mrg[:, 2:4], ACT.Exp).then_inc(e["scales"], 1)
                            act.wait_ge(e["merged"], done("merged", k))
                            act.dma_start(rows, st_out[:, :]).then_inc(e["stored"], 16)
                            act.wait_ge(e["stored"], k * 16 + 16)

        def sum_pass(table, total):
            with nc.Block() as block:
                @block.gpsimd
                def _(pool):
                    gather_chunks(pool, table, D)

                @block.tensor
                def _(pe):
                    start_counts(pe, "summed")
                    with pe.Fori(0, C // 2) as i:
                        for j in range(2):
                            k = i * 2 + j
                            pe.wait_ge(e["hot"], done("hot", k))
                            pe.wait_ge(e[f"rows{j}"], i * (16 * G) + 16 * G)
                            pe.wait_ge(e["merged"], done("merged", k - 1))
                            for t in range(G):
                                last = pe.matmul(ps_a[0:W, 0:D], onehot[:, t, :], g[:, j, t, 0:D],
                                                 start=(t == 0), stop=(t == G - 1))
                            last.then_inc(e["summed"], 1)

                @block.vector
                def _(dve):
                    start_counts(dve, "hot", "merged")
                    with dve.Fori(0, C // 2) as i:
                        for j in range(2):
                            k = i * 2 + j
                            dve.wait_ge(e["summed"], done("summed", k - 1))
                            dve.tensor_tensor(onehot[:, :, :], per_edge(dcol[:, bass.ds(k * G, G)]),
                                              iota_rows(), ALU.is_equal).then_inc(e["hot"], 1)
                            dve.wait_ge(e["state"], k * 16 + 16)
                            dve.wait_ge(e["summed"], done("summed", k))
                            dve.tensor_tensor(st_out[:, 0:D], st_in[:, 0:D], ps_a[0:W, 0:D],
                                              ALU.add).then_inc(e["merged"], 1)

                @block.scalar
                def _(act):
                    with act.Fori(0, C // 2) as i:
                        for j in range(2):
                            k = i * 2 + j
                            add_window(act, total, k)

        def add_window(act, total, k):
            rows = total[bass.ds(window_of(act, k), W), :]
            act.dma_start(st_in[:, 0:D], rows).then_inc(e["state"], 16)
            act.wait_ge(e["merged"], done("merged", k))
            act.dma_start(rows, st_out[:, 0:D]).then_inc(e["stored"], 16)
            act.wait_ge(e["stored"], k * 16 + 16)

        def message_pass():
            with nc.Block() as block:
                @block.gpsimd
                def _(pool):
                    gather_chunks(pool, h_rows[1], D)

                @block.sync
                def _(sp):
                    with sp.Fori(0, C // 2) as i:
                        for j in range(2):
                            k = i * 2 + j
                            window = window_of(sp, k)
                            sp.wait_ge(e["hot"], done("hot", k - 2))
                            sp.sem_inc(e["loading"], 1)
                            sp.dma_start(drow[:, j, :], rel_rows[bass.ds(k, 1), :]
                                         .to_broadcast([W, EC])).then_inc(e[f"rel{j}"], 16)
                            sp.wait_ge(e["dst"], done("dst", k - 2))
                            sp.sem_inc(e["loading"], 1)
                            sp.dma_start(lhs[W:W + D_EDGE, j, :], ea32_t[:, bass.ds(k * EC, EC)]
                                         ).then_inc(e[f"attr{j}"], 16)
                            sp.dma_start(win[0:W, j, :], win_rows[1][bass.ds(window, W), :]
                                         ).then_inc(e[f"win{j}"], 16)

                @block.tensor
                def _(pe):
                    start_counts(pe, "dst", "summed")
                    with pe.Fori(0, C // 2) as i:
                        for j in range(2):
                            k = i * 2 + j
                            pe.wait_ge(e["hot"], done("hot", k))
                            pe.wait_ge(e[f"attr{j}"], i * 16 + 16)
                            pe.wait_ge(e[f"win{j}"], i * 16 + 16)
                            pe.wait_ge(e["score"], done("score", k - 1))
                            for t in range(G):
                                last = pe.matmul(ps_x[:, t, :], lhs[:, j, t * P:(t + 1) * P],
                                                 win[:, j, :], start=True, stop=True)
                            last.then_inc(e["dst"], 1)
                            pe.wait_ge(e["p"], k + 1)
                            pe.wait_ge(e["merged"], done("merged", k - 1))
                            for t in range(G):
                                last = pe.matmul(ps_a[0:W, 0:D], onehot[:, t, :], weighted[:, t, :],
                                                 start=(t == 0), stop=(t == G - 1))
                            last.then_inc(e["summed"], 1)

                @block.vector
                def _(dve):
                    start_counts(dve, "hot", "merged", "score")
                    with dve.Fori(0, C // 2) as i:
                        for j in range(2):
                            k = i * 2 + j
                            dve.wait_ge(e["summed"], done("summed", k - 1))
                            dve.tensor_tensor(onehot[:, :, :], per_edge(dcol[:, bass.ds(k * G, G)]),
                                              iota_rows(), ALU.is_equal)
                            dve.wait_ge(e[f"rel{j}"], i * 16 + 16)
                            dve.tensor_scalar(lhs[0:W, j, :], drow[:, j, :], iota_col[0:W, 1:2], None,
                                              ALU.is_equal).then_inc(e["hot"], 1)
                            dve.wait_ge(e[f"rows{j}"], i * (16 * G) + 16 * G)
                            dve.wait_ge(e["dst"], done("dst", k))
                            dve.tensor_tensor(weighted[:, :, :], g[:, j, :, 0:D], ps_x[:, 0:G, :],
                                              ALU.add).then_inc(e["score"], 1)
                            dve.wait_ge(e["state"], k * 16 + 16)
                            dve.wait_ge(e["summed"], done("summed", k))
                            dve.tensor_tensor(st_out[:, 0:D], st_in[:, 0:D], ps_a[0:W, 0:D],
                                              ALU.add).then_inc(e["merged"], 1)

                @block.scalar
                def _(act):
                    with act.Fori(0, C // 2) as i:
                        for j in range(2):
                            k = i * 2 + j
                            rows = sums[1][bass.ds(window_of(act, k), W), :]
                            act.dma_start(st_in[:, 0:D], rows).then_inc(e["state"], 16)
                            act.wait_ge(e["score"], done("score", k))
                            act.activation(weighted[:, :, :], weighted[:, :, :], ACT.Relu
                                           ).then_inc(e["p"], 1)
                            act.wait_ge(e["merged"], done("merged", k))
                            act.dma_start(rows, st_out[:, 0:D]).then_inc(e["stored"], 16)
                            act.wait_ge(e["stored"], k * 16 + 16)

        layernorm_relu()
        norm, inv = col[:, 0, :], col[:, 1, :]
        with nc.Block() as block:
            @block.vector
            def _(dve):
                link(dve, dve.tensor_tensor(tmp[:, :, :], h[:, :, :], h[:, :, :], ALU.mult))
                link(dve, dve.tensor_reduce(norm, tmp[:, :, :], AX.X, ALU.add))
                counts["squares"] = at(s_vec)
                link(dve, dve.tensor_copy(state[:, :, 0:D], h[:, :, :]))
                link(dve, dve.memset(state[:, :, D:D + 1], 1.0))
                dve.wait_ge(s_act, at(s_act) + 1)
                link(dve, dve.tensor_scalar(norm, norm, 1e-12, None, ALU.max))
                link(dve, dve.reciprocal(inv, norm))
                link(dve, dve.tensor_copy(state[:, :, D + 1:D + 2], col[:, 1, :].rearrange("p (t o) -> p t o", o=1)))
                link(dve, dve.tensor_tensor(tmp[:, :, :], h[:, :, :], per_node(inv), ALU.mult))

            @block.scalar
            def _(act):
                act.wait_ge(s_vec, counts["squares"])
                bump(s_act, act.activation(norm, norm, ACT.Sqrt))

        store_rows([(node_rows(h0_rows, ROW0), state[:, :, 0:ROW0]), (node_rows(win_rows[0], D), tmp[:, :, :])])
        over_windows(attention_pass)
        load_rows(state, node_rows(state0, ST0))
        degree = col[:, 2, :]
        with nc.Block() as block:
            @block.vector
            def _(dve):
                link(dve, dve.tensor_scalar(norm, state[:, :, S_DEN], 1.2e-38, None, ALU.max))
                link(dve, dve.reciprocal(inv, norm))
                link(dve, dve.tensor_tensor(tmp[:, :, :], state[:, :, 0:D], per_node(inv), ALU.mult))
                link(dve, dve.tensor_tensor(x[:, :, :], x[:, :, :], tmp[:, :, :], ALU.add))
                link(dve, dve.tensor_scalar(degree, state[:, :, S_DEG], 1.0, None, ALU.max))
                link(dve, dve.reciprocal(degree, degree))

        layernorm_relu()
        store_rows([(node_rows(h_rows[0], D), h[:, :, :])])
        over_windows(lambda: sum_pass(h_rows[0], sums[0]))
        load_rows(tmp[:, :, :], node_rows(sums[0], D))
        with nc.Block() as block:
            @block.vector
            def _(dve):
                link(dve, dve.tensor_tensor(tmp[:, :, :], tmp[:, :, :], state[:, :, S_EA:S_EA + D], ALU.add))
                link(dve, dve.tensor_tensor(tmp[:, :, :], tmp[:, :, :], per_node(degree), ALU.mult))
                link(dve, dve.tensor_scalar(stat[:, 5:6], par[:, 7:8], 1.0, None, ALU.add))
                link(dve, dve.scalar_tensor_tensor(tmp[:, :, :], h[:, :, :], stat[:, 5:6], tmp[:, :, :],
                                                   ALU.mult, ALU.add))
        transpose_nodes(tmp, D, hT[0:D, :])
        project(w1_sb[:, :], hT[0:D, :], y1t, par[:, 0:1], par[:, 1:2], par[:, 2:3], P, bn1)
        project(w2_sb[:, :], y1t, hT[0:D, :], par[0:D, 3:4], par[0:D, 4:5], par[0:D, 5:6], D, bn1)
        with nc.Block() as block:
            pe0, vec0 = at(s_pe), at(s_vec)
            by_node = hT[0:D, :].rearrange("f (p t) -> f t p", t=NT)
            starts = list(range(0, NT, 8))

            @block.tensor
            def _(pe):
                for n, t0 in enumerate(starts):
                    if n >= 2:
                        pe.wait_ge(s_vec, vec0 + n - 1)
                    for t in range(t0, min(t0 + 8, NT)):
                        last = pe.transpose(banks[n % 2][:, (t - t0) * D:(t - t0 + 1) * D], by_node[:, t, :],
                                            ident[0:D, 0:D])
                    bump(s_pe, last)

            @block.vector
            def _(dve):
                for n, t0 in enumerate(starts):
                    dve.wait_ge(s_pe, pe0 + n + 1)
                    k = min(8, NT - t0)
                    bump(s_vec, dve.tensor_tensor(
                        x[:, t0:t0 + k, :], x[:, t0:t0 + k, :],
                        banks[n % 2][:, 0:k * D].rearrange("p (t f) -> p t f", f=D), ALU.add))
                dve.wait_ge(s_vec, at(s_vec))

        layernorm_relu()
        transpose_nodes(h, D, hT[0:D, :])
        with nc.Block() as block:
            pe0, vec0 = at(s_pe), at(s_vec)
            hT_nodes = hT[0:D + 1, :].rearrange("f (p t) -> f t p", t=NT)
            pq = arena[:, 0:NT * 2 * D].rearrange("p (t f) -> p t f", f=2 * D)
            starts = list(range(0, NT, 4))

            @block.tensor
            def _(pe):
                pe.wait_ge(s_vec, vec0 + 1)
                for n, t0 in enumerate(starts):
                    if n >= 2:
                        pe.wait_ge(s_vec, vec0 + n)
                    for t in range(t0, min(t0 + 4, NT)):
                        last = pe.matmul(banks[n % 2][:, (t - t0) * P:(t - t0 + 1) * P], hT_nodes[:, t, :],
                                         wsd_sb[:, :], start=True, stop=True)
                    bump(s_pe, last)

            @block.vector
            def _(dve):
                bump(s_vec, dve.memset(hT[D:D + 1, :], 1.0))
                for n, t0 in enumerate(starts):
                    dve.wait_ge(s_pe, pe0 + n + 1)
                    k = min(4, NT - t0)
                    bump(s_vec, dve.tensor_copy(
                        pq[:, t0:t0 + k, :], banks[n % 2][:, 0:k * P].rearrange("p (t f) -> p t f", f=P)))
                dve.wait_ge(s_vec, at(s_vec))

        store_rows([(node_rows(h_rows[1], D), pq[:, :, 0:D]), (node_rows(win_rows[1], D), pq[:, :, D:2 * D])])
        over_windows(message_pass)
        load_rows(tmp[:, :, :], node_rows(sums[1], D))
        with nc.Block() as block:
            @block.vector
            def _(dve):
                link(dve, dve.tensor_tensor(cat[:, :, 0:D], tmp[:, :, :], per_node(degree), ALU.mult))
                link(dve, dve.tensor_copy(cat[:, :, D:2 * D], h[:, :, :]))
        transpose_nodes(cat, 2 * D, hT[:, :])
        with nc.Block() as block:
            pe0, vec0 = at(s_pe), at(s_vec)
            cat_nodes = hT[:, :].rearrange("f (p t) -> f t p", t=NT)
            starts = list(range(0, NT, 8))

            @block.tensor
            def _(pe):
                for n, t0 in enumerate(starts):
                    if n >= 2:
                        pe.wait_ge(s_vec, vec0 + n - 1)
                    for t in range(t0, min(t0 + 8, NT)):
                        last = pe.matmul(banks[n % 2][:, (t - t0) * D:(t - t0 + 1) * D], cat_nodes[:, t, :],
                                         wv_sb[:, :], start=True, stop=True)
                    bump(s_pe, last)

            @block.vector
            def _(dve):
                for n, t0 in enumerate(starts):
                    dve.wait_ge(s_pe, pe0 + n + 1)
                    k = min(8, NT - t0)
                    bump(s_vec, dve.tensor_tensor(
                        tmp[:, t0:t0 + k, :], banks[n % 2][:, 0:k * D].rearrange("p (t f) -> p t f", f=D),
                        bv_sb[:, :].rearrange("p (o f) -> p o f", o=1).to_broadcast([P, k, D]), ALU.add))
                dve.wait_ge(s_vec, at(s_vec))
                link(dve, dve.scalar_tensor_tensor(x[:, :, :], tmp[:, :, :], 0.0, x[:, :, :], ALU.max, ALU.add))

        layernorm_relu()
        store_rows([(node_rows(h_rows[2], D), h[:, :, :])])
        over_windows(lambda: sum_pass(h_rows[2], sums[2]))
        load_rows(tmp[:, :, :], node_rows(sums[2], D))
        with nc.Block() as block:
            @block.vector
            def _(dve):
                link(dve, dve.tensor_tensor(x[:, :, :], x[:, :, :], tmp[:, :, :], ALU.add))
                counts["x"] = at(s_vec)

            @block.sync
            def _(sp):
                sp.wait_ge(s_vec, counts["x"])
                bump(s_store, sp.dma_start(out.rearrange("(p t) f -> p t f", t=NT), x[:, :, :]), 16)
                sp.wait_ge(s_store, at(s_store))


def kernel(**inputs):
    import concourse.bacc as bacc
    from concourse.bass_utils import run_bass_kernel_spmd

    arrays = lay_out(inputs)
    nc = bacc.Bacc("TRN2", target_bir_lowering=False, num_devices=1)
    args = [nc.dram_tensor(name, a.shape, mybir.dt.from_np(a.dtype), kind="ExternalInput").ap()
            for name, a in arrays.items()]
    out = nc.dram_tensor("out", (NPAD, D), F32, kind="ExternalOutput").ap()
    gnn_layers(nc, *args, out)
    r = run_bass_kernel_spmd(nc, [arrays], core_ids=[0])
    return r.results[0]["out"][0:N]


def lay_out(inputs):
    a = {k: np.ascontiguousarray(v) for k, v in inputs.items()}
    pad = T * P - E

    def edges(v, fill=0):
        return np.concatenate([v, np.full((pad, *v.shape[1:]), fill, v.dtype)])

    dst = edges(a["dst"].astype(np.int32), NO_NODE)
    arrays = {
        "x_in": np.concatenate([a["x"], np.zeros((NPAD - N, D), np.float32)]),
        "src_c": edges(a["src"].astype(np.int32)).reshape(T, P).T,
        "dst_c": dst.reshape(T, P).T,
        "dst_r": dst.reshape(C, EC),
        "ea32_t": edges(a["edge_attr_32"]).T,
        "ea64_c": edges(a["edge_attr_64"]).reshape(C, G, P, D).transpose(0, 2, 1, 3),
        "beta": a["L0_gnn_beta"], "eps": a["L1_gnn_eps"],
        "w1": a["L1_gnn_W1"], "b1": a["L1_gnn_b1"], "gamma1": a["L1_gnn_gamma1"], "beta1": a["L1_gnn_beta1"],
        "w2": a["L1_gnn_W2"], "b2": a["L1_gnn_b2"], "gamma2": a["L1_gnn_gamma2"], "beta2": a["L1_gnn_beta2"],
        "w_e": a["L2_gnn_W_e"], "b_e": a["L2_gnn_b_e"], "w_v": a["L2_gnn_W_v"], "b_v": a["L2_gnn_b_v"],
    }
    return {k: np.ascontiguousarray(v) for k, v in arrays.items()}
```

```python
import numpy as np
import concourse.bass as bass
from concourse import mybir
from contextlib import ExitStack

F32 = mybir.dt.float32
I32 = mybir.dt.int32
I16 = mybir.dt.int16
F16 = mybir.dt.float16
ALU = mybir.AluOpType
ACT = mybir.ActivationFunctionType
AX = mybir.AxisListType

N, E, D = 6250, 206250, 64
D_EDGE = 32
P = 128
NT = -(-N // P)
NPAD = P * NT
NROWS = NPAD + P
G = 14
C = -(-E // (P * G))
NS = 4
GROUPS = C // NS
T = C * G
EC = G * P
W = 64
NO_NODE = 16384
MAX_PASSES = N // W + 1
BIG = 1.0e30
LN_EPS = BN_EPS = 1e-5
ROW0 = D + 2
ST0 = 2 * D + 3
S_DEN, S_MAX, S_EA, S_DEG = D, D + 1, D + 2, 2 * D + 2
NQ = -(-NPAD // 512)
PAIRS = T // 2
CP = G // 2
PW = 12
PH = PW // 2
CW = W + PW
NB = 224
SPLIT = 2.0 ** 11
assert C % NS == 0 and NS % 2 == 0 and N + W <= NROWS and G % 2 == 0 and NPAD % (2 * NB) == 0


def gnn_layers(nc, x_in, src_c, dst_c, dst_r, ea32_t, ea64_c, beta, eps, w1, b1, gamma1, beta1,
               w2, b2, gamma2, beta2, w_e, b_e, w_v, b_v, out):
    ctx = ExitStack()
    with ctx:
        def sb(name, shape, dt=F32):
            return ctx.enter_context(nc.sbuf_tensor(name, shape, dt))

        def ps(name, shape):
            return ctx.enter_context(nc.psum_tensor(name, shape, F32))

        def sem(name):
            return ctx.enter_context(nc.semaphore(name))

        def dram(name, shape, dt=F32):
            return nc.dram_tensor(name, shape, dt, kind="Internal").ap()

        h0_rows = dram("h0_rows", (NPAD, ROW0))
        h_rows = [dram(f"h_rows{i}", (NPAD, D)) for i in range(3)]
        win_rows = [dram(f"win_rows{i}", (NROWS, D)) for i in range(2)]
        state0 = dram("state0", (NROWS, ST0))
        sums = [dram(f"sums{i}", (NROWS, D)) for i in range(3)]
        span_d = dram("span_d", (C, 2))
        rel_rows = dram("rel_rows", (C, EC), I16)
        pair_d = dram("pair_d", (2, PAIRS))
        edge_counts = dram("edge_counts", (P, NROWS * NT), F16)

        x = sb("x", [P, NT, D])
        h = sb("h", [P, NT, D])
        h_flat = h[:, :, :].rearrange("p t f -> p (t f)")
        tmp = sb("tmp", [P, NT, D])
        arena = sb("arena", [P, NT * ST0])
        state = arena[:, :].rearrange("p (t f) -> p t f", f=ST0)
        cat = arena[:, 0:NT * 2 * D].rearrange("p (t f) -> p t f", f=2 * D)
        y1t = arena[:, 0:NPAD]
        hT = sb("hT", [P, NPAD])
        ident = sb("ident", [P, P])
        halves = sb("halves", [P, D])
        dense = sb("dense", [1, 1], I32)
        tests = sb("tests", [1, 8])
        col = sb("col", [P, 8, NT])
        w1_sb = sb("w1_sb", [D, 2 * D])
        w2_sb = sb("w2_sb", [2 * D, D])
        wsd_sb = sb("wsd_sb", [D + 1, 2 * D])
        wv_sb = sb("wv_sb", [2 * D, D])
        bv_sb = sb("bv_sb", [P, D])
        par = sb("par", [P, 8])
        bn1 = sb("bn1", [P, NQ, 6])
        bna = sb("bna", [P, 8])
        src_sb = sb("src_sb", [P, T], I32)
        dcol = sb("dcol", [P, T])
        iota_row = sb("iota_row", [P, 2, W])
        iota_col = sb("iota_col", [P, 2])
        base0 = sb("base0", [1, C], I32)
        base = sb("base", [1, C], I32)
        spans = sb("spans", [P, C, 2])
        stat = sb("stat", [P, 8])
        stat2 = sb("stat2", [P, 2 * CP])
        passes = sb("passes", [1, 2], I32)
        idx = sb("idx", [P, NS, G], I32)
        g = sb("g", [P, NS, G, ROW0])
        onehot = sb("onehot", [P, 2, G, W])
        weighted = sb("weighted", [P, G, W])
        product = sb("product", [P, G, W])
        edge_space = sb("edge_space", [P, 4 * EC])
        lhs = edge_space[0:W + D_EDGE, 0:2 * EC].rearrange("w (s e) -> w s e", s=2)
        off_window = edge_space[0:W, 2 * EC:4 * EC].rearrange("w (s e) -> w s e", s=2)
        drow = sb("drow", [W, 2, EC], I16)
        ea = sb("ea", [P, 2, G, D + 1])
        win = sb("win", [W + D_EDGE, 2, D])
        sc = sb("sc", [P, 2, 4, G])
        st_in = sb("st_in", [W, ST0])
        st_out = sb("st_out", [W, ST0])
        mrg = sb("mrg", [W, 2, 8])
        rel16 = weighted[:, :, :].rearrange("p g w -> p (g w)").bitcast(I16)[:, 0:EC]
        key, key_next, src_row = hT[:, 0:T], hT[:, T:2 * T], hT[:, 2 * T:3 * T]
        pair_min, pair_max = h_flat[:, 0:PAIRS + 2], h_flat[0:1, PAIRS + 2:2 * PAIRS + 2]
        offset = h_flat[0:1, 2 * PAIRS + 2:3 * PAIRS + 2].bitcast(I32)
        quotient, dst, place = (edge_space[:, i * T:(i + 1) * T] for i in range(3))
        iota_wide, offset_f = edge_space[:, 3 * T:3 * T + PW * NT], edge_space[0:1, 3 * T + 600:3 * T + 600 + PAIRS]
        one16 = tmp[:, :, :].rearrange("p t f -> p (t f)").bitcast(F16)
        iota16 = one16[:, 0:PW * NT]
        hot_dst = one16[:, 600:600 + 4 * PW * NT].rearrange("p (s n) -> p s n", s=4)
        hot_next = one16[:, 3000:3000 + 4 * CP * NT].rearrange("p (s n) -> p s n", s=4 * CP)
        hot_src = arena[:, 3840:3840 + 2 * CP * P].bitcast(F16).rearrange("p (s n) -> p s n", s=4 * CP)
        chunk_counts = [arena[:, i * 1920:i * 1920 + CW * NT // 2].bitcast(F16) for i in range(2)]
        parts = g[:, :, :, :].rearrange("p s g f -> p (s g f)").bitcast(F16)[:, 0:NT * 2 * D] \
            .rearrange("p (t f) -> p t f", f=2 * D)
        blocks = [space.bitcast(F16).rearrange("p (w a) -> p w a", a=NT)
                  for space in (arena[:, 0:NB * NT // 2], edge_space[:, 0:NB * NT // 2])]
        ps_x = ps("ps_x", [P, 16, W])
        ps_t = ps("ps_t", [P, 16, P])
        ps_a = ps("ps_a", [P, 512])
        ps_b = ps("ps_b", [P, 512])
        banks = [ps_t[:, 4 * i:4 * i + 4, :].rearrange("p a b -> p (a b)") for i in range(4)]

        def iota_rows():
            return iota_row[:, 1, :].rearrange("p (o w) -> p o w", o=1).to_broadcast([P, G, W])

        def per_edge(a):
            return a.rearrange("p (g o) -> p g o", o=1).to_broadcast([P, G, W])

        def per_node(a):
            return a.rearrange("p (t o) -> p t o", o=1).to_broadcast([P, NT, D])

        def node_rows(table, width):
            return table[0:NPAD, 0:width].rearrange("(p t) f -> p t f", t=NT)

        s_load = sem("s_load")
        s_vec = sem("s_vec")
        s_act = sem("s_act")
        s_pool = sem("s_pool")
        s_pe = sem("s_pe")
        s_store = sem("s_store")
        s_spans = sem("s_spans")
        s_pairs = sem("s_pairs")
        c_made, c_counted, c_copied = sem("c_made"), sem("c_counted"), sem("c_copied")
        c_stored = sem("c_stored")
        d_loaded = [sem("d_loaded0"), sem("d_loaded1")]
        d_split, d_parts, d_product, d_copied = sem("d_split"), sem("d_parts"), sem("d_product"), sem("d_copied")
        d_rows, d_added = sem("d_rows"), sem("d_added")
        d_fetched, d_gathered = sem("d_fetched"), sem("d_gathered")

        counts = {}

        def bump(which, ins, by=1):
            ins.then_inc(which, by)
            counts[which.name] = counts.get(which.name, 0) + by
            return counts.get(which.name, 0)

        def at(which):
            return counts.get(which.name, 0)

        def link(eng, ins):
            eng.wait_ge(s_vec, bump(s_vec, ins))

        with nc.Block() as block:
            @block.sync
            def _(sp):
                def load(dst, src):
                    bump(s_load, sp.dma_start(dst, src), 16)

                load(x[:, :, :], x_in.rearrange("(p t) f -> p t f", t=NT))
                load(src_sb[:, :], src_c)
                load(arena[:, 0:T].bitcast(I32), dst_c)
                load(hT[0:C, 0:EC].bitcast(I32), dst_r)
                with nc.allow_non_contiguous_dma("a value per partition"):
                    load(par[:, 0:1], b1.rearrange("(p o) -> p o", o=1))
                    load(par[:, 1:2], gamma1.rearrange("(p o) -> p o", o=1))
                    load(par[:, 2:3], beta1.rearrange("(p o) -> p o", o=1))
                    load(par[0:D, 3:4], b2.rearrange("(p o) -> p o", o=1))
                    load(par[0:D, 4:5], gamma2.rearrange("(p o) -> p o", o=1))
                    load(par[0:D, 5:6], beta2.rearrange("(p o) -> p o", o=1))
                    load(par[:, 6:7], beta.rearrange("(p o) -> p o", o=1).to_broadcast([P, 1]))
                    load(par[:, 7:8], eps.rearrange("(p o) -> p o", o=1).to_broadcast([P, 1]))
                load(w1_sb[:, :], w1)
                load(w2_sb[:, :], w2)
                load(wsd_sb[0:D, 0:D], w_e[0:D, :])
                load(wsd_sb[0:D, D:2 * D], w_e[D + D_EDGE:2 * D + D_EDGE, :])
                load(wsd_sb[D:D + 1, D:2 * D], b_e.rearrange("(o f) -> o f", o=1))
                for j in range(2):
                    load(win[W:W + D_EDGE, j, :], w_e[D:D + D_EDGE, :])
                load(wv_sb[:, :], w_v)
                load(bv_sb[:, :], b_v.rearrange("(o f) -> o f", o=1).to_broadcast([P, D]))

            @block.gpsimd
            def _(pool):
                pool.memset(ident[:, :], 0.0).then_inc(s_pool, 1)
                pool.wait_ge(s_pool, 1)
                pool.affine_select(out=ident[:, :], in_=ident[:, :], compare_op=ALU.not_equal, fill=1.0,
                                   base=0, pattern=[[-1, P]], channel_multiplier=1).then_inc(s_pool, 1)
                pool.iota(iota_row[:, 0, :], pattern=[[1, W]], base=0, channel_multiplier=0,
                          allow_small_or_imprecise_dtypes=True).then_inc(s_pool, 1)
                pool.iota(iota_col[:, 0:1], pattern=[[0, 1]], base=0, channel_multiplier=1,
                          allow_small_or_imprecise_dtypes=True).then_inc(s_pool, 1)
                pool.wait_ge(s_pool, 4)

            @block.vector
            def _(dve):
                dve.memset(ea[:, :, :, D:D + 1], 1.0)
                dve.memset(wsd_sb[D:D + 1, 0:D], 0.0)
                link(dve, dve.memset(tmp[:, :, :], 0.0))
                dve.wait_ge(s_load, at(s_load))

        with nc.Block() as block:
            @block.vector
            def _(dve):
                dst, dstf, real = hT[0:C, 0:EC].bitcast(I32), hT[0:C, 2048:2048 + EC], hT[0:C, 4096:4096 + EC]
                link(dve, dve.tensor_copy(dstf, dst))
                link(dve, dve.tensor_reduce(stat[0:C, 0:1], dstf, AX.X, ALU.min))
                link(dve, dve.tensor_scalar(real, dstf, float(N), None, ALU.is_lt))
                link(dve, dve.tensor_tensor(real, dstf, real, ALU.mult))
                link(dve, dve.tensor_reduce(stat[0:C, 2:3], real, AX.X, ALU.max))
                link(dve, dve.tensor_tensor(stat[0:C, 1:2], stat[0:C, 2:3], stat[0:C, 0:1], ALU.subtract))
                counts["spans known"] = at(s_vec)
                link(dve, dve.tensor_scalar(rel16[0:C, :], dstf, stat[0:C, 0:1], None, ALU.subtract))
                counts["rows relative"] = at(s_vec)
                pairs = [v.rearrange("c (q e) -> c q e", q=CP) for v in (dstf, real)]
                link(dve, dve.tensor_reduce(stat2[0:C, 0:CP], pairs[0], AX.X, ALU.min))
                link(dve, dve.tensor_scalar(stat2[0:C, 0:CP], stat2[0:C, 0:CP], float(N), None, ALU.min))
                link(dve, dve.tensor_reduce(stat2[0:C, CP:2 * CP], pairs[1], AX.X, ALU.max))
                counts["pairs known"] = at(s_vec)
                dve.wait_ge(s_spans, 16)
                link(dve, dve.tensor_copy(base0[0:1, :], spans[0:1, :, 0]))
                link(dve, dve.tensor_reduce(stat[0:1, 4:5], spans[0:1, :, 1], AX.X, ALU.max))
                link(dve, dve.tensor_copy(passes[0:1, 0:1], stat[0:1, 4:5]))
                link(dve, dve.tensor_scalar(passes[0:1, 0:1], passes[0:1, 0:1], W.bit_length() - 1, None,
                                            ALU.arith_shift_right))
                link(dve, dve.tensor_scalar(passes[0:1, 1:2], passes[0:1, 0:1], 1.0, None, ALU.add))
                link(dve, dve.tensor_copy(dcol[:, 0:T], arena[:, 0:T].bitcast(I32)))
                link(dve, dve.tensor_tensor(
                    dcol[:, 0:T].rearrange("p (c g) -> p c g", g=G),
                    dcol[:, 0:T].rearrange("p (c g) -> p c g", g=G),
                    spans[:, :, 0:1].to_broadcast([P, C, G]), ALU.subtract))

            @block.sync
            def _(sp):
                sp.wait_ge(s_vec, counts["spans known"])
                sp.dma_start(span_d, stat[0:C, 0:2]).then_inc(s_store, 16)
                sp.wait_ge(s_store, 16)
                sp.dma_start(spans[:, :, :], span_d.rearrange("(o c) f -> o c f", o=1)
                             .to_broadcast([P, C, 2])).then_inc(s_spans, 16)
                sp.wait_ge(s_vec, counts["rows relative"])
                sp.dma_start(rel_rows[0:C, :], rel16[0:C, :]).then_inc(s_store, 16)
                sp.wait_ge(s_vec, counts["pairs known"])
                for i in range(2):
                    sp.dma_start(pair_d[i:i + 1, :].rearrange("o (c q) -> (o c) q", q=CP),
                                 stat2[0:C, i * CP:(i + 1) * CP]).then_inc(s_store, 16)
                sp.wait_ge(s_store, 64)
                counts[s_store.name] = 64
                sp.dma_start(pair_min[:, 0:PAIRS], pair_d[0:1, :].to_broadcast([P, PAIRS])).then_inc(s_pairs, 16)
                sp.dma_start(pair_max, pair_d[1:2, :]).then_inc(s_pairs, 16)
                sp.wait_ge(s_pairs, 32)

        with nc.Block() as block:
            @block.vector
            def _(dve):
                link(dve, dve.memset(arena[:, :], 0.0))
                link(dve, dve.memset(state[:, :, S_MAX:S_MAX + 1], -BIG))
                counts["zeroed"] = at(s_vec)

            @block.sync
            def _(sp):
                sp.wait_ge(s_vec, counts["zeroed"])
                bump(s_store, sp.dma_start(node_rows(state0, ST0), state), 16)
                bump(s_store, sp.dma_start(state0[NPAD:NROWS, :], state[:, 0, :]), 16)
                bump(s_store, sp.dma_start(edge_counts[:, N * NT:NPAD * NT],
                                           tmp[:, :, :].rearrange("p t f -> p (t f)").bitcast(F16)
                                           [:, 0:(NPAD - N) * NT]), 16)
                for table in sums + win_rows:
                    bump(s_store, sp.dma_start(node_rows(table, D), tmp[:, :, :]), 16)
                    bump(s_store, sp.dma_start(table[NPAD:NROWS, :], tmp[:, 0, :]), 16)
                sp.wait_ge(s_store, at(s_store))

        def layernorm_relu():
            mean, var = col[:, 0, :], col[:, 1, :]
            with nc.Block() as block:
                @block.vector
                def _(dve):
                    link(dve, dve.tensor_reduce(mean, x[:, :, :], AX.X, ALU.add))
                    link(dve, dve.tensor_scalar(mean, mean, 1.0 / D, None, ALU.mult))
                    link(dve, dve.tensor_tensor(h[:, :, :], x[:, :, :], per_node(mean), ALU.subtract))
                    link(dve, dve.tensor_tensor(tmp[:, :, :], h[:, :, :], h[:, :, :], ALU.mult))
                    link(dve, dve.tensor_reduce(var, tmp[:, :, :], AX.X, ALU.add))
                    link(dve, dve.tensor_scalar(var, var, 1.0 / D, LN_EPS, ALU.mult, ALU.add))
                    counts["variance"] = at(s_vec)
                    dve.wait_ge(s_act, at(s_act) + 1)
                    link(dve, dve.reciprocal(var, var))
                    link(dve, dve.tensor_tensor(h[:, :, :], h[:, :, :], per_node(var), ALU.mult))
                    link(dve, dve.tensor_scalar(h[:, :, :], h[:, :, :], 0.0, None, ALU.max))

                @block.scalar
                def _(act):
                    act.wait_ge(s_vec, counts["variance"])
                    bump(s_act, act.activation(var, var, ACT.Sqrt))

        def transpose_nodes(rows, width, to):
            first, done = at(s_pe), at(s_vec)
            by_node = to.rearrange("f (p t) -> f t p", t=NT)
            starts = list(range(0, NT, 4))
            with nc.Block() as block:
                @block.tensor
                def _(pe):
                    for n, t0 in enumerate(starts):
                        if n >= 2:
                            pe.wait_ge(s_vec, done + n - 1)
                        for t in range(t0, min(t0 + 4, NT)):
                            last = pe.transpose(banks[n % 2][0:width, (t - t0) * P:(t - t0 + 1) * P],
                                                rows[:, t, :], ident[:, :])
                        bump(s_pe, last)

                @block.vector
                def _(dve):
                    for n, t0 in enumerate(starts):
                        dve.wait_ge(s_pe, first + n + 1)
                        k = min(4, NT - t0)
                        bump(s_vec, dve.tensor_copy(
                            by_node[:, t0:t0 + k, :],
                            banks[n % 2][0:width, 0:k * P].rearrange("f (t p) -> f t p", t=k)))
                    dve.wait_ge(s_vec, at(s_vec))

        def project(weights, rows_in, to, bias, gamma, shift, width, stats):
            pe0, act0 = at(s_pe), at(s_act)
            mv, scale = bna[0:width, 0:2], bna[0:width, 2:3]
            with nc.Block() as block:
                @block.tensor
                def _(pe):
                    for q in range(NQ):
                        n = min(512, NPAD - 512 * q)
                        if q >= 2:
                            pe.wait_ge(s_act, act0 + q - 1)
                        bump(s_pe, pe.matmul(banks[q % 2][0:width, 0:n], weights,
                                             rows_in[:, 512 * q:512 * q + n], start=True, stop=True))

                @block.scalar
                def _(act):
                    for q in range(NQ):
                        n = min(512, NPAD - 512 * q)
                        act.wait_ge(s_pe, pe0 + q + 1)
                        bump(s_act, act.activation(to[:, 512 * q:512 * q + n], banks[q % 2][0:width, 0:n],
                                                   ACT.Identity, bias=bias))

                @block.vector
                def _(dve):
                    for q in range(NQ):
                        n = min(512, N - 512 * q)
                        dve.wait_ge(s_act, act0 + q + 1)
                        link(dve, dve.bn_stats(stats[0:width, q, :], to[:, 512 * q:512 * q + n]))
                    link(dve, dve.bn_aggr(mv, stats[0:width, :, :].rearrange("p q s -> p (q s)")))
                    link(dve, dve.tensor_scalar(scale, mv[:, 1:2], BN_EPS, None, ALU.add))
                    counts["variance"] = at(s_vec)

            with nc.Block() as block:
                @block.vector
                def _(dve):
                    dve.wait_ge(s_act, at(s_act) + 1)
                    link(dve, dve.reciprocal(scale, scale))
                    link(dve, dve.tensor_tensor(scale, scale, gamma, ALU.mult))
                    link(dve, dve.tensor_tensor(bna[0:width, 3:4], mv[:, 0:1], scale, ALU.mult))
                    link(dve, dve.tensor_tensor(bna[0:width, 4:5], shift, bna[0:width, 3:4], ALU.subtract))
                    counts["affine"] = at(s_vec)

                @block.scalar
                def _(act):
                    bump(s_act, act.activation(scale, scale, ACT.Sqrt))
                    act.wait_ge(s_vec, counts["affine"])
                    bump(s_act, act.activation(to, to, ACT.Relu, scale=scale, bias=bna[0:width, 4:5]))
                    act.wait_ge(s_act, at(s_act))

        def store_rows(pairs):
            with nc.Block() as block:
                @block.sync
                def _(sp):
                    for table, rows in pairs:
                        bump(s_store, sp.dma_start(table, rows), 16)
                    sp.wait_ge(s_store, at(s_store))

        def load_rows(rows, table):
            with nc.Block() as block:
                @block.sync
                def _(sp):
                    bump(s_load, sp.dma_start(rows, table), 16)
                    sp.wait_ge(s_load, at(s_load))

        e = {name: sem("e_" + name) for name in (
            "idx", "gathering", "reducing", "loading", "product", "columns", "dot", "new_top", "scaled", "spreading", "rows0", "rows1", "rows2", "rows3", "rel0", "rel1", "attr0", "attr1", "win0", "win1", "hot", "dst",
            "score", "spread", "top", "topped", "lowered", "p", "weighted", "summed", "attr_summed",
            "state", "pair", "scales", "merged", "stored")}
        START = {"hot": 2, "dst": 2, "summed": 4, "attr_summed": 2, "topped": 2,
                 "lowered": 1, "merged": 1, "top": 1, "score": 1, "product": 1}

        def done(name, k):
            return k + 1 + START.get(name, 0)

        def start_counts(eng, *names):
            for name in names:
                eng.sem_inc(e[name], START[name])

        def start_windows():
            with nc.Block() as block:
                @block.vector
                def _(dve):
                    bump(s_vec, dve.tensor_copy(base[:, :], base0[:, :]))
                    bump(s_vec, dve.tensor_copy(iota_row[:, 1, :], iota_row[:, 0, :]))
                    link(dve, dve.tensor_copy(iota_col[:, 1:2], iota_col[:, 0:1]))

        def next_windows():
            with nc.Block() as block:
                @block.vector
                def _(dve):
                    dve.tensor_scalar(base[:, :], base[:, :], float(W), float(N), ALU.add, ALU.min)
                    dve.tensor_scalar(iota_row[:, 1, :], iota_row[:, 1, :], float(W), None, ALU.add)
                    dve.tensor_scalar(iota_col[:, 1:2], iota_col[:, 1:2], float(W), None, ALU.add)

        def over_windows(one_pass):
            start_windows()
            n = nc.values_load(passes[0:1, 1:2], min_val=1, max_val=MAX_PASSES)
            with nc.Fori(0, n):
                nc.gpsimd.dma_reset()
                nc.all_engine_barrier()
                for s in e.values():
                    nc.sync.sem_clear(s)
                nc.all_engine_barrier()
                one_pass()
                next_windows()

        def gather_chunks(pool, table, width):
            with pool.Fori(0, GROUPS) as i:
                for j in range(NS):
                    k = i * NS + j
                    pool.wait_ge(e["summed"], done("summed", k - NS))
                    pool.tensor_copy(idx[:, j, :], src_sb[:, bass.ds(k * G, G)]).then_inc(e["idx"], 1)
                    pool.wait_ge(e["idx"], k + 1)
                    pool.sem_inc(e["gathering"], 1)
                    for t in range(G):
                        pool.indirect_dma_start(
                            g[:, j, t, 0:width], None, table,
                            bass.IndirectOffsetOnAxis(ap=idx[:, j, t:t + 1], axis=0)
                        ).then_inc(e[f"rows{j}"], 16)
            for j in range(NS):
                pool.wait_ge(e[f"rows{j}"], GROUPS * G * 16)

        def window_of(eng, k):
            return eng.value_load(base[0:1, bass.ds(k, 1)], min_val=0, max_val=N)

        def attention_pass():
            def loads(i, j):
                return i * (NS * 8) + j // 2 * 16 + 16

            def over_chunks(eng, step):
                with eng.Fori(0, GROUPS - 1) as i:
                    for j in range(NS):
                        step(i, j, True)
                for j in range(NS):
                    step(GROUPS - 1, j, j < NS - 1)

            with nc.Block() as block:
                @block.gpsimd
                def _(pool):
                    gather_chunks(pool, h0_rows, ROW0)

                @block.sync
                def _(sp):
                    with sp.Fori(0, GROUPS) as i:
                        for j in range(NS):
                            k, s = i * NS + j, j % 2
                            window = window_of(sp, k)
                            sp.wait_ge(e["hot"], done("hot", k - 2))
                            sp.sem_inc(e["loading"], 1)
                            sp.dma_start(drow[:, s, :], rel_rows[bass.ds(k, 1), :]
                                         .to_broadcast([W, EC])).then_inc(e[f"rel{s}"], 16)
                            sp.wait_ge(e["dst"], done("dst", k - 2))
                            sp.sem_inc(e["loading"], 1)
                            sp.dma_start(win[0:W, s, :], win_rows[0][bass.ds(window, W), :]
                                         ).then_inc(e[f"win{s}"], 16)
                            sp.wait_ge(e["attr_summed"], done("attr_summed", k - 2))
                            sp.sem_inc(e["loading"], 1)
                            sp.dma_start(ea[:, s, :, 0:D], ea64_c[bass.ds(k, 1), :, :, :]
                                         .rearrange("o p g f -> (o p) g f")).then_inc(e[f"attr{s}"], 16)

                @block.tensor
                def _(pe):
                    start_counts(pe, "dst", "summed", "attr_summed", "topped")

                    def spread_rows(i, j):
                        k, s = i * NS + j, j % 2
                        pe.wait_ge(e["hot"], done("hot", k))
                        pe.wait_ge(e[f"win{s}"], loads(i, j))
                        pe.wait_ge(e["product"], done("product", k - 1))
                        for t in range(G):
                            last = pe.matmul(ps_x[:, t, :], lhs[0:W, s, t * P:(t + 1) * P],
                                             win[0:W, s, :], start=True, stop=True)
                        last.then_inc(e["dst"], 1)

                    def spread_scores(i, j):
                        k, s = i * NS + j, j % 2
                        pe.wait_ge(e["top"], done("top", k - 1))
                        pe.wait_ge(e["score"], done("score", k))
                        pe.sem_inc(e["spreading"], 1)
                        for t in range(G):
                            last = pe.transpose(ps_t[0:W, t, :], sc[:, s, 0, t:t + 1].to_broadcast([P, W]),
                                                ident[:, :])
                        last.then_inc(e["spread"], 1)

                    def step(i, j, more):
                        k, s = i * NS + j, j % 2
                        pe.wait_ge(e["merged"], done("merged", k - 1))
                        pe.wait_ge(e["top"], done("top", k))
                        for t in range(G):
                            last = pe.matmul(ps_a[:, P + t:P + t + 1], lhs[0:W, s, t * P:(t + 1) * P],
                                             mrg[:, s, 0:1], start=True, stop=True)
                        last.then_inc(e["topped"], 1)
                        if more:
                            spread_rows(i + (j + 1) // NS, (j + 1) % NS)
                        pe.wait_ge(e["columns"], k + 1)
                        pe.wait_ge(e[f"attr{s}"], loads(i, j))
                        for t in range(G):
                            last = pe.matmul(ps_b[0:W, 0:D + 1], onehot[:, s, t, :], ea[:, s, t, :],
                                             start=(t == 0), stop=(t == G - 1))
                        last.then_inc(e["attr_summed"], 1)
                        pe.wait_ge(e["weighted"], k + 1)
                        for t in range(G):
                            last = pe.matmul(ps_a[0:W, 0:D + 1], weighted[:, t, :], g[:, j, t, 0:D + 1],
                                             start=(t == 0), stop=(t == G - 1))
                        last.then_inc(e["summed"], 1)
                        if more:
                            spread_scores(i + (j + 1) // NS, (j + 1) % NS)

                    spread_rows(0, 0)
                    spread_scores(0, 0)
                    over_chunks(pe, step)

                @block.vector
                def _(dve):
                    start_counts(dve, "hot", "lowered", "merged", "top", "score", "product")

                    def one_hots(i, j):
                        k, s = i * NS + j, j % 2
                        dve.wait_ge(e["topped"], done("topped", k - 2))
                        dve.wait_ge(e[f"rel{s}"], loads(i, j))
                        dve.tensor_scalar(lhs[0:W, s, :], drow[:, s, :], iota_col[0:W, 1:2], None,
                                          ALU.is_equal)
                        dve.tensor_scalar(off_window[:, s, :], drow[:, s, :], iota_col[0:W, 1:2], -BIG,
                                          ALU.not_equal, ALU.mult).then_inc(e["hot"], 1)

                    def scores(i, j):
                        k, s = i * NS + j, j % 2
                        dve.wait_ge(e[f"rows{j}"], i * (16 * G) + 16 * G)
                        dve.wait_ge(e["dst"], done("dst", k))
                        dve.tensor_tensor(product[:, :, :], g[:, j, :, 0:D], ps_x[:, 0:G, :],
                                          ALU.mult).then_inc(e["product"], 1)
                        dve.wait_ge(e["product"], done("product", k))
                        dve.tensor_reduce(sc[:, s, 1, :], product[:, :, :], AX.X, ALU.add
                                          ).then_inc(e["dot"], 1)
                        dve.wait_ge(e["dot"], k + 1)
                        dve.scalar_tensor_tensor(sc[:, s, 0, :], sc[:, s, 1, :], par[:, 6:7],
                                                 g[:, j, :, D + 1], ALU.mult, ALU.mult
                                                 ).then_inc(e["score"], 1)

                    def maxima(i, j):
                        k, s = i * NS + j, j % 2
                        dve.wait_ge(e["spread"], k + 1)
                        dve.sem_inc(e["reducing"], 1)
                        dve.tensor_tensor_reduce(
                            out=off_window[:, s, :].rearrange("w (g p) -> w g p", p=P),
                            in0=ps_t[0:W, 0:G, :],
                            in1=off_window[:, s, :].rearrange("w (g p) -> w g p", p=P),
                            scale=1.0, scalar=-BIG, op0=ALU.add, op1=ALU.max,
                            accum_out=mrg[:, s, 0:1]).then_inc(e["top"], 1)

                    def step(i, j, more):
                        k, s = i * NS + j, j % 2
                        i1, j1 = i + (j + 1) // NS, (j + 1) % NS
                        dve.wait_ge(e["attr_summed"], done("attr_summed", k - 2))
                        dve.tensor_tensor(onehot[:, s, :, :], per_edge(dcol[:, bass.ds(k * G, G)]),
                                          iota_rows(), ALU.is_equal).then_inc(e["columns"], 1)
                        dve.wait_ge(e["topped"], done("topped", k))
                        dve.tensor_tensor(sc[:, s, 2, :], sc[:, s, 0, :], ps_a[:, P:P + G],
                                          ALU.subtract).then_inc(e["lowered"], 1)
                        dve.wait_ge(e["summed"], done("summed", k - 1))
                        dve.wait_ge(e["p"], k + 1)
                        dve.tensor_tensor(weighted[:, :, :], onehot[:, s, :, :], per_edge(sc[:, s, 3, :]),
                                          ALU.mult).then_inc(e["weighted"], 1)
                        if more:
                            scores(i1, j1)
                        if more and not (type(i) is int and j == NS - 2):
                            one_hots(i + (j + 2) // NS, (j + 2) % NS)
                        dve.wait_ge(e["state"], k * 16 + 16)
                        dve.wait_ge(e["top"], done("top", k))
                        dve.tensor_tensor(mrg[:, s, 1:2], mrg[:, s, 0:1], st_in[:, S_MAX:S_MAX + 1],
                                          ALU.max).then_inc(e["new_top"], 1)
                        dve.wait_ge(e["new_top"], k + 1)
                        dve.tensor_tensor(mrg[:, s, 2:3], st_in[:, S_MAX:S_MAX + 1], mrg[:, s, 1:2],
                                          ALU.subtract)
                        dve.tensor_tensor(mrg[:, s, 3:4], mrg[:, s, 0:1], mrg[:, s, 1:2],
                                          ALU.subtract).then_inc(e["pair"], 1)
                        dve.wait_ge(e["scales"], k + 1)
                        dve.tensor_scalar(st_out[:, 0:D + 1], st_in[:, 0:D + 1], mrg[:, s, 4:5], None,
                                          ALU.mult).then_inc(e["scaled"], 1)
                        dve.tensor_copy(st_out[:, S_MAX:S_MAX + 1], mrg[:, s, 1:2])
                        dve.wait_ge(e["attr_summed"], done("attr_summed", k))
                        dve.tensor_tensor(st_out[:, S_EA:ST0], st_in[:, S_EA:ST0],
                                          ps_b[0:W, 0:D + 1], ALU.add)
                        dve.wait_ge(e["summed"], done("summed", k))
                        dve.wait_ge(e["scaled"], k + 1)
                        dve.scalar_tensor_tensor(st_out[:, 0:D + 1], ps_a[0:W, 0:D + 1], mrg[:, s, 5:6],
                                                 st_out[:, 0:D + 1], ALU.mult, ALU.add
                                                 ).then_inc(e["merged"], 1)
                        if more:
                            maxima(i1, j1)

                    one_hots(0, 0)
                    one_hots(0, 1)
                    scores(0, 0)
                    maxima(0, 0)
                    over_chunks(dve, step)

                @block.scalar
                def _(act):
                    with act.Fori(0, GROUPS) as i:
                        for j in range(NS):
                            k, s = i * NS + j, j % 2
                            rows = state0[bass.ds(window_of(act, k), W), :]
                            act.dma_start(st_in[:, :], rows).then_inc(e["state"], 16)
                            act.wait_ge(e["lowered"], done("lowered", k))
                            act.activation(sc[:, s, 3, :], sc[:, s, 2, :], ACT.Exp).then_inc(e["p"], 1)
                            act.wait_ge(e["pair"], k + 1)
                            act.activation(mrg[:, s, 4:6], mrg[:, s, 2:4], ACT.Exp).then_inc(e["scales"], 1)
                            act.wait_ge(e["merged"], done("merged", k))
                            act.dma_start(rows, st_out[:, :]).then_inc(e["stored"], 16)
                            act.wait_ge(e["stored"], k * 16 + 16)

        def is_dense(eng):
            return eng.value_load(dense[0:1, 0:1], min_val=0, max_val=1)

        def sum_pass(table, total):
            with nc.Block() as block:
                @block.gpsimd
                def _(pool):
                    with pool.If(is_dense(pool) == 0):
                        gather_chunks(pool, table, D)

                @block.tensor
                def _(pe):
                    with pe.If(is_dense(pe) == 0):
                        start_counts(pe, "summed")
                        with pe.Fori(0, GROUPS) as i:
                            for j in range(NS):
                                k = i * NS + j
                                pe.wait_ge(e["hot"], done("hot", k))
                                pe.wait_ge(e[f"rows{j}"], i * (16 * G) + 16 * G)
                                pe.wait_ge(e["merged"], done("merged", k - 1))
                                for t in range(G):
                                    last = pe.matmul(ps_a[0:W, 0:D], onehot[:, j % 2, t, :], g[:, j, t, 0:D],
                                                     start=(t == 0), stop=(t == G - 1))
                                last.then_inc(e["summed"], 1)

                @block.vector
                def _(dve):
                    with dve.If(is_dense(dve) == 0):
                        start_counts(dve, "hot", "merged")
                        with dve.Fori(0, GROUPS) as i:
                            for j in range(NS):
                                k = i * NS + j
                                dve.wait_ge(e["summed"], done("summed", k - 1))
                                dve.tensor_tensor(onehot[:, j % 2, :, :], per_edge(dcol[:, bass.ds(k * G, G)]),
                                                  iota_rows(), ALU.is_equal).then_inc(e["hot"], 1)
                                dve.wait_ge(e["state"], k * 16 + 16)
                                dve.wait_ge(e["summed"], done("summed", k))
                                dve.tensor_tensor(st_out[:, 0:D], st_in[:, 0:D], ps_a[0:W, 0:D],
                                                  ALU.add).then_inc(e["merged"], 1)

                @block.scalar
                def _(act):
                    with act.If(is_dense(act) == 0):
                        with act.Fori(0, GROUPS) as i:
                            for j in range(NS):
                                add_window(act, total, i * NS + j)

        def add_window(act, total, k):
            rows = total[bass.ds(window_of(act, k), W), :]
            act.dma_start(st_in[:, 0:D], rows).then_inc(e["state"], 16)
            act.wait_ge(e["merged"], done("merged", k))
            act.dma_start(rows, st_out[:, 0:D]).then_inc(e["stored"], 16)
            act.wait_ge(e["stored"], k * 16 + 16)

        def message_pass():
            with nc.Block() as block:
                @block.gpsimd
                def _(pool):
                    gather_chunks(pool, h_rows[1], D)

                @block.sync
                def _(sp):
                    with sp.Fori(0, GROUPS) as i:
                        for j in range(NS):
                            k = i * NS + j
                            window = window_of(sp, k)
                            sp.wait_ge(e["hot"], done("hot", k - 2))
                            sp.sem_inc(e["loading"], 1)
                            sp.dma_start(drow[:, j % 2, :], rel_rows[bass.ds(k, 1), :]
                                         .to_broadcast([W, EC])).then_inc(e[f"rel{j % 2}"], 16)
                            sp.wait_ge(e["dst"], done("dst", k - 2))
                            sp.sem_inc(e["loading"], 1)
                            sp.dma_start(lhs[W:W + D_EDGE, j % 2, :], ea32_t[:, bass.ds(k * EC, EC)]
                                         ).then_inc(e[f"attr{j % 2}"], 16)
                            sp.dma_start(win[0:W, j % 2, :], win_rows[1][bass.ds(window, W), :]
                                         ).then_inc(e[f"win{j % 2}"], 16)

                @block.tensor
                def _(pe):
                    start_counts(pe, "dst", "summed")
                    with pe.Fori(0, GROUPS) as i:
                        for j in range(NS):
                            k = i * NS + j
                            pe.wait_ge(e["hot"], done("hot", k))
                            pe.wait_ge(e[f"attr{j % 2}"], i * (NS * 8) + j // 2 * 16 + 16)
                            pe.wait_ge(e[f"win{j % 2}"], i * (NS * 8) + j // 2 * 16 + 16)
                            pe.wait_ge(e["score"], done("score", k - 1))
                            for t in range(G):
                                last = pe.matmul(ps_x[:, t, :], lhs[:, j % 2, t * P:(t + 1) * P],
                                                 win[:, j % 2, :], start=True, stop=True)
                            last.then_inc(e["dst"], 1)
                            pe.wait_ge(e["p"], k + 1)
                            pe.wait_ge(e["merged"], done("merged", k - 1))
                            for t in range(G):
                                last = pe.matmul(ps_a[0:W, 0:D], onehot[:, j % 2, t, :], weighted[:, t, :],
                                                 start=(t == 0), stop=(t == G - 1))
                            last.then_inc(e["summed"], 1)

                @block.vector
                def _(dve):
                    start_counts(dve, "hot", "merged", "score")
                    with dve.Fori(0, GROUPS) as i:
                        for j in range(NS):
                            k = i * NS + j
                            dve.wait_ge(e["summed"], done("summed", k - 1))
                            dve.tensor_tensor(onehot[:, j % 2, :, :], per_edge(dcol[:, bass.ds(k * G, G)]),
                                              iota_rows(), ALU.is_equal)
                            dve.wait_ge(e[f"rel{j % 2}"], i * (NS * 8) + j // 2 * 16 + 16)
                            dve.tensor_scalar(lhs[0:W, j % 2, :], drow[:, j % 2, :], iota_col[0:W, 1:2], None,
                                              ALU.is_equal).then_inc(e["hot"], 1)
                            dve.wait_ge(e[f"rows{j}"], i * (16 * G) + 16 * G)
                            dve.wait_ge(e["dst"], done("dst", k))
                            dve.tensor_tensor(weighted[:, :, :], g[:, j, :, 0:D], ps_x[:, 0:G, :],
                                              ALU.add).then_inc(e["score"], 1)
                            dve.wait_ge(e["state"], k * 16 + 16)
                            dve.wait_ge(e["summed"], done("summed", k))
                            dve.tensor_tensor(st_out[:, 0:D], st_in[:, 0:D], ps_a[0:W, 0:D],
                                              ALU.add).then_inc(e["merged"], 1)

                @block.scalar
                def _(act):
                    with act.Fori(0, GROUPS) as i:
                        for j in range(NS):
                            k = i * NS + j
                            rows = sums[1][bass.ds(window_of(act, k), W), :]
                            act.dma_start(st_in[:, 0:D], rows).then_inc(e["state"], 16)
                            act.wait_ge(e["score"], done("score", k))
                            act.activation(weighted[:, :, :], weighted[:, :, :], ACT.Relu
                                           ).then_inc(e["p"], 1)
                            act.wait_ge(e["merged"], done("merged", k))
                            act.dma_start(rows, st_out[:, 0:D]).then_inc(e["stored"], 16)
                            act.wait_ge(e["stored"], k * 16 + 16)

        with nc.Block() as block:
            @block.gpsimd
            def _(pool):
                pool.iota(iota_wide, pattern=[[1, PW * NT]], base=0, channel_multiplier=0,
                          allow_small_or_imprecise_dtypes=True).then_inc(s_pool, 1)

            @block.vector
            def _(dve):
                first, second, third = pair_min[:, 0:PAIRS], pair_min[:, 1:PAIRS + 1], pair_min[:, 2:PAIRS + 2]
                link(dve, dve.memset(pair_min[:, PAIRS:PAIRS + 2], float(N)))

                def test(place, left, right, most):
                    n = left.shape[-1]
                    link(dve, dve.tensor_tensor(offset_f[:, 0:n], left, right, ALU.subtract))
                    link(dve, dve.tensor_reduce(tests[:, place:place + 1], offset_f[:, 0:n], AX.X, ALU.max))
                    link(dve, dve.tensor_scalar(tests[:, place:place + 1], tests[:, place:place + 1],
                                                float(most), None, ALU.subtract))

                test(0, second[0:1, :], first[0:1, :], PW)
                test(1, pair_max, first[0:1, :], PW - 1)
                test(2, pair_max, second[0:1, :], 0)
                test(3, pair_max, third[0:1, :], -1)
                chunk_ends = pair_min[0:1, CP:PAIRS + 1:CP]
                test(4, chunk_ends, pair_min[0:1, 0:PAIRS:CP], W)
                link(dve, dve.tensor_copy(tests[:, 5:6], first[0:1, 0:1]))
                link(dve, dve.tensor_reduce(tests[:, 6:7], tests[:, 0:6], AX.X, ALU.max))
                link(dve, dve.tensor_scalar(tests[:, 6:7], tests[:, 6:7], 0.0, None, ALU.is_le))
                link(dve, dve.tensor_copy(dense[:, :], tests[:, 6:7]))
                link(dve, dve.tensor_tensor(
                    offset_f.rearrange("o (c q) -> o c q", q=CP),
                    first[0:1, :].rearrange("o (c q) -> o c q", q=CP),
                    spans[0:1, :, 0:1].to_broadcast([1, C, CP]), ALU.subtract))
                link(dve, dve.tensor_scalar(offset_f, offset_f, 0.0, float(W), ALU.max, ALU.min))
                link(dve, dve.tensor_copy(offset, offset_f))
                whole = quotient.bitcast(I32)
                link(dve, dve.tensor_copy(key, src_sb[:, :]))
                link(dve, dve.tensor_scalar(src_row, key, 1.0 / NT, None, ALU.mult))
                link(dve, dve.tensor_copy(whole, src_row))
                link(dve, dve.tensor_copy(src_row, whole))
                link(dve, dve.scalar_tensor_tensor(key, src_row, -float(NT), key, ALU.mult, ALU.add))
                for wrong, step in ((ALU.is_lt, -1.0), (ALU.is_ge, 1.0)):
                    link(dve, dve.tensor_scalar(key_next, key, 0.0 if step < 0 else float(NT), step,
                                                wrong, ALU.mult))
                    link(dve, dve.tensor_tensor(src_row, src_row, key_next, ALU.add))
                    link(dve, dve.scalar_tensor_tensor(key, key_next, -float(NT), key, ALU.mult, ALU.add))
                link(dve, dve.tensor_tensor(
                    dst.rearrange("p (c g) -> p c g", g=G), dcol[:, :].rearrange("p (c g) -> p c g", g=G),
                    spans[:, :, 0:1].to_broadcast([P, C, G]), ALU.add))
                for to, mins in ((key_next, second), (key, first)):
                    link(dve, dve.tensor_tensor(
                        place.rearrange("p (q s) -> p q s", s=2), dst.rearrange("p (q s) -> p q s", s=2),
                        mins.rearrange("p (q o) -> p q o", o=1).to_broadcast([P, PAIRS, 2]), ALU.subtract))
                    link(dve, dve.scalar_tensor_tensor(to, place, float(NT), key, ALU.mult, ALU.add))
                dve.wait_ge(s_pool, 5)
                link(dve, dve.tensor_copy(iota16, iota_wide))
                link(dve, dve.memset(one16[:, 600:6000], 0.0))
                link(dve, dve.scalar_tensor_tensor(halves[:, :], ident[:, D:2 * D], 1.0 / SPLIT, ident[:, 0:D],
                                                   ALU.mult, ALU.add))

        with nc.Block() as block:
            @block.vector
            def _(dve):
                link(dve, dve.memset(arena[:, 0:3840 + 2 * CP * P], 0.0))

        with nc.Block() as block:
            @block.vector
            def _(dve):
                with dve.Fori(0, C // 2) as i:
                    for u in range(2 * CP):
                        q = i * (2 * CP) + u
                        dve.wait_ge(c_counted, q + 1)
                        for s in range(2):
                            t, slot = q * 2 + s, 2 * u + s
                            dve.tensor_scalar(hot_dst[:, 2 * (u % 2) + s, :], iota16, key[:, bass.ds(t, 1)],
                                              None, ALU.is_equal)
                            dve.tensor_scalar(hot_next[:, slot, :], iota16[:, 0:NT],
                                              key_next[:, bass.ds(t, 1)], None, ALU.is_equal)
                            last = dve.tensor_scalar(hot_src[:, slot, :], iota16[:, 0:P],
                                                     src_row[:, bass.ds(t, 1)], None, ALU.is_equal)
                        last.then_inc(c_made, 1)

            @block.tensor
            def _(pe):
                pe.sem_inc(c_counted, 2)
                with pe.Fori(0, C // 2) as i:
                    for u in range(2 * CP):
                        q = i * (2 * CP) + u
                        to = ps_t[:, 8 * (u % 2):8 * (u % 2) + 8, :].rearrange("p (b x) c -> p b (x c)", b=2)
                        pe.wait_ge(c_made, q + 1)
                        pe.wait_ge(c_copied, q + 1)
                        for s in range(2):
                            for b in range(2):
                                last = pe.matmul(to[:, b, 0:PH * NT], hot_src[:, 2 * u + s, :],
                                                 hot_dst[:, 2 * (u % 2) + s, b * PH * NT:(b + 1) * PH * NT],
                                                 start=(s == 0), stop=(s == 1))
                            if s == 0:
                                for before in ((2 * u - 2) % (4 * CP), (2 * u - 1) % (4 * CP)):
                                    pe.matmul(to[:, 0, 0:NT], hot_src[:, before, :], hot_next[:, before, :],
                                              start=False, stop=False)
                        last.then_inc(c_counted, 1)

            @block.scalar
            def _(act):
                act.sem_inc(c_copied, 2)
                act.sem_inc(c_stored, 32)
                with act.Fori(0, C // 2) as i:
                    for u in range(2 * CP):
                        q = i * (2 * CP) + u
                        if u % CP == 0:
                            act.wait_ge(c_stored, (i * 2 + u // CP) * 16 + 16)
                        start = act.value_load(offset[0:1, bass.ds(q, 1)], min_val=0, max_val=W)
                        act.wait_ge(c_copied, q + 2)
                        act.wait_ge(c_counted, q + 3)
                        act.activation(
                            chunk_counts[u // CP][:, bass.ds(start * NT, PW * NT)]
                            .rearrange("p (b n) -> p b n", b=2),
                            ps_t[:, 8 * (u % 2):8 * (u % 2) + 8, :].rearrange("p (b x) c -> p b (x c)", b=2)
                            [:, :, 0:PH * NT], ACT.Copy).then_inc(c_copied, 1)

            @block.sync
            def _(sp):
                with sp.Fori(0, C // 2) as i:
                    for u in range(2):
                        c = i * 2 + u
                        window = sp.value_load(base0[0:1, bass.ds(c, 1)], min_val=0, max_val=N)
                        sp.wait_ge(c_copied, c * CP + CP + 2)
                        sp.wait_ge(c_stored, c * 16 + 32)
                        sp.dma_start(edge_counts[:, bass.ds(window * NT, W * NT)],
                                     chunk_counts[u][:, 0:W * NT]).then_inc(c_stored, 16)
                sp.wait_ge(c_stored, C * 16 + 32)

        def sum_neighbours(table, total):
            blocks_done, rows_done, added_done = at(d_product), at(d_rows), at(d_added)
            copied0, parts0, split0 = at(d_copied), at(d_parts), at(d_split)
            loads0, fetched0 = at(d_loaded[0]), at(d_fetched)
            n_blocks = NPAD // NB
            sums_rows = arena[:, 0:NT * D].rearrange("p (t f) -> p t f", f=D)
            low = hT[:, 0:NT * D].rearrange("p (t f) -> p t f", f=D)
            by_node = hT[:, :].rearrange("f (p t) -> f t p", t=NT)
            starts = list(range(0, NT, 8))

            with nc.Block() as block:
                @block.sync
                def _(sp):
                    with sp.If(is_dense(sp) == 1):
                        with sp.Fori(0, n_blocks // 2) as i:
                            for s in range(2):
                                sp.wait_ge(d_product, i * 2 + (blocks_done + s + 1))
                                sp.sem_inc(d_fetched, 1)
                                sp.dma_start(blocks[s].rearrange("p w a -> p (w a)"),
                                             edge_counts[:, bass.ds(i * (2 * NB * NT) + s * NB * NT, NB * NT)]
                                             ).then_inc(d_loaded[s], 16)

                @block.vector
                def _(dve):
                    with dve.If(is_dense(dve) == 1):
                        dve.tensor_copy(parts[:, :, 0:D], h[:, :, :]).then_inc(d_split, 1)
                        dve.wait_ge(d_split, split0 + 1)
                        dve.tensor_tensor(low, h[:, :, :], parts[:, :, 0:D], ALU.subtract).then_inc(d_split, 1)
                        dve.wait_ge(d_split, split0 + 2)
                        dve.tensor_scalar(parts[:, :, D:2 * D], low, SPLIT, None, ALU.mult).then_inc(d_split, 1)
                        dve.wait_ge(d_split, split0 + 3)
                        dve.sem_inc(d_parts, 1)
                        with dve.Fori(0, n_blocks // 2) as i:
                            for s in range(2):
                                dve.wait_ge(d_product, i * 2 + (blocks_done + s + 3))
                                dve.tensor_copy(hT[:, bass.ds(i * (2 * NB) + s * NB, NB)],
                                                banks[s][:, 0:NB]).then_inc(d_copied, 1)

                @block.tensor
                def _(pe):
                    with pe.If(is_dense(pe) == 1):
                        pe.sem_inc(d_product, 2)
                        pe.wait_ge(d_parts, parts0 + 1)
                        with pe.Fori(0, n_blocks // 2) as i:
                            for s in range(2):
                                pe.wait_ge(d_loaded[s], i * 16 + (loads0 + 16))
                                pe.wait_ge(d_copied, i * 2 + (copied0 + s + 1))
                                for a in range(NT):
                                    last = pe.matmul(banks[s][:, 0:NB], parts[:, a, :], blocks[s][:, :, a],
                                                     start=(a == 0), stop=(a == NT - 1))
                                last.then_inc(d_product, 1)

                @block.scalar
                def _(act):
                    with act.If(is_dense(act) == 1):
                        act.sem_inc(d_copied, 2)
            for name, by in ((d_product, n_blocks + 2), (d_copied, n_blocks + 2), (d_parts, 1), (d_split, 3),
                             (d_loaded[0], n_blocks // 2 * 16), (d_fetched, n_blocks)):
                counts[name.name] = counts.get(name.name, 0) + by

            with nc.Block() as block:
                @block.tensor
                def _(pe):
                    with pe.If(is_dense(pe) == 1):
                        for n, t0 in enumerate(starts):
                            if n >= 2:
                                pe.wait_ge(d_added, added_done + n - 1)
                            for t in range(t0, min(t0 + 8, NT)):
                                last = pe.matmul(banks[n % 2][:, (t - t0) * D:(t - t0 + 1) * D],
                                                 by_node[:, t, :], halves[:, :], start=True, stop=True)
                            last.then_inc(d_rows, 1)

                @block.vector
                def _(dve):
                    with dve.If(is_dense(dve) == 1):
                        for n, t0 in enumerate(starts):
                            dve.wait_ge(d_rows, rows_done + n + 1)
                            k = min(8, NT - t0)
                            dve.tensor_copy(sums_rows[:, t0:t0 + k, :], banks[n % 2][:, 0:k * D]
                                            .rearrange("p (t f) -> p t f", f=D)).then_inc(d_added, 1)
                        dve.wait_ge(d_added, added_done + len(starts))

            for name in (d_rows, d_added):
                counts[name.name] = counts.get(name.name, 0) + len(starts)

            store_rows([(node_rows(table, D), h[:, :, :])])
            over_windows(lambda: sum_pass(table, total))
            with nc.Block() as block:
                @block.sync
                def _(sp):
                    with sp.If(is_dense(sp) == 0):
                        sp.dma_start(sums_rows, node_rows(total, D)).then_inc(d_gathered, 16)
                        sp.wait_ge(d_gathered, at(d_gathered) + 16)
            counts[d_gathered.name] = at(d_gathered) + 16
            return sums_rows

        layernorm_relu()
        norm, inv = col[:, 0, :], col[:, 1, :]
        with nc.Block() as block:
            @block.vector
            def _(dve):
                link(dve, dve.tensor_tensor(tmp[:, :, :], h[:, :, :], h[:, :, :], ALU.mult))
                link(dve, dve.tensor_reduce(norm, tmp[:, :, :], AX.X, ALU.add))
                counts["squares"] = at(s_vec)
                link(dve, dve.tensor_copy(state[:, :, 0:D], h[:, :, :]))
                link(dve, dve.memset(state[:, :, D:D + 1], 1.0))
                dve.wait_ge(s_act, at(s_act) + 1)
                link(dve, dve.tensor_scalar(norm, norm, 1e-12, None, ALU.max))
                link(dve, dve.reciprocal(inv, norm))
                link(dve, dve.tensor_copy(state[:, :, D + 1:D + 2], col[:, 1, :].rearrange("p (t o) -> p t o", o=1)))
                link(dve, dve.tensor_tensor(tmp[:, :, :], h[:, :, :], per_node(inv), ALU.mult))

            @block.scalar
            def _(act):
                act.wait_ge(s_vec, counts["squares"])
                bump(s_act, act.activation(norm, norm, ACT.Sqrt))

        store_rows([(node_rows(h0_rows, ROW0), state[:, :, 0:ROW0]), (node_rows(win_rows[0], D), tmp[:, :, :])])
        over_windows(attention_pass)
        load_rows(state, node_rows(state0, ST0))
        degree = col[:, 2, :]
        with nc.Block() as block:
            @block.vector
            def _(dve):
                link(dve, dve.tensor_scalar(norm, state[:, :, S_DEN], 1.2e-38, None, ALU.max))
                link(dve, dve.reciprocal(inv, norm))
                link(dve, dve.tensor_tensor(tmp[:, :, :], state[:, :, 0:D], per_node(inv), ALU.mult))
                link(dve, dve.tensor_tensor(x[:, :, :], x[:, :, :], tmp[:, :, :], ALU.add))
                link(dve, dve.tensor_scalar(degree, state[:, :, S_DEG], 1.0, None, ALU.max))
                link(dve, dve.reciprocal(degree, degree))

        layernorm_relu()
        with nc.Block() as block:
            @block.vector
            def _(dve):
                link(dve, dve.tensor_copy(tmp[:, :, :], state[:, :, S_EA:S_EA + D]))
        neighbours = sum_neighbours(h_rows[0], sums[0])
        with nc.Block() as block:
            @block.vector
            def _(dve):
                link(dve, dve.tensor_tensor(tmp[:, :, :], tmp[:, :, :], neighbours, ALU.add))
                link(dve, dve.tensor_tensor(tmp[:, :, :], tmp[:, :, :], per_node(degree), ALU.mult))
                link(dve, dve.tensor_scalar(stat[:, 5:6], par[:, 7:8], 1.0, None, ALU.add))
                link(dve, dve.scalar_tensor_tensor(tmp[:, :, :], h[:, :, :], stat[:, 5:6], tmp[:, :, :],
                                                   ALU.mult, ALU.add))
        transpose_nodes(tmp, D, hT[0:D, :])
        project(w1_sb[:, :], hT[0:D, :], y1t, par[:, 0:1], par[:, 1:2], par[:, 2:3], P, bn1)
        project(w2_sb[:, :], y1t, hT[0:D, :], par[0:D, 3:4], par[0:D, 4:5], par[0:D, 5:6], D, bn1)
        with nc.Block() as block:
            pe0, vec0 = at(s_pe), at(s_vec)
            by_node = hT[0:D, :].rearrange("f (p t) -> f t p", t=NT)
            starts = list(range(0, NT, 8))

            @block.tensor
            def _(pe):
                for n, t0 in enumerate(starts):
                    if n >= 2:
                        pe.wait_ge(s_vec, vec0 + n - 1)
                    for t in range(t0, min(t0 + 8, NT)):
                        last = pe.transpose(banks[n % 2][:, (t - t0) * D:(t - t0 + 1) * D], by_node[:, t, :],
                                            ident[0:D, 0:D])
                    bump(s_pe, last)

            @block.vector
            def _(dve):
                for n, t0 in enumerate(starts):
                    dve.wait_ge(s_pe, pe0 + n + 1)
                    k = min(8, NT - t0)
                    bump(s_vec, dve.tensor_tensor(
                        x[:, t0:t0 + k, :], x[:, t0:t0 + k, :],
                        banks[n % 2][:, 0:k * D].rearrange("p (t f) -> p t f", f=D), ALU.add))
                dve.wait_ge(s_vec, at(s_vec))

        layernorm_relu()
        transpose_nodes(h, D, hT[0:D, :])
        with nc.Block() as block:
            pe0, vec0 = at(s_pe), at(s_vec)
            hT_nodes = hT[0:D + 1, :].rearrange("f (p t) -> f t p", t=NT)
            pq = arena[:, 0:NT * 2 * D].rearrange("p (t f) -> p t f", f=2 * D)
            starts = list(range(0, NT, 4))

            @block.tensor
            def _(pe):
                pe.wait_ge(s_vec, vec0 + 1)
                for n, t0 in enumerate(starts):
                    if n >= 2:
                        pe.wait_ge(s_vec, vec0 + n)
                    for t in range(t0, min(t0 + 4, NT)):
                        last = pe.matmul(banks[n % 2][:, (t - t0) * P:(t - t0 + 1) * P], hT_nodes[:, t, :],
                                         wsd_sb[:, :], start=True, stop=True)
                    bump(s_pe, last)

            @block.vector
            def _(dve):
                bump(s_vec, dve.memset(hT[D:D + 1, :], 1.0))
                for n, t0 in enumerate(starts):
                    dve.wait_ge(s_pe, pe0 + n + 1)
                    k = min(4, NT - t0)
                    bump(s_vec, dve.tensor_copy(
                        pq[:, t0:t0 + k, :], banks[n % 2][:, 0:k * P].rearrange("p (t f) -> p t f", f=P)))
                dve.wait_ge(s_vec, at(s_vec))

        store_rows([(node_rows(h_rows[1], D), pq[:, :, 0:D]), (node_rows(win_rows[1], D), pq[:, :, D:2 * D])])
        over_windows(message_pass)
        load_rows(tmp[:, :, :], node_rows(sums[1], D))
        with nc.Block() as block:
            @block.vector
            def _(dve):
                link(dve, dve.tensor_tensor(cat[:, :, 0:D], tmp[:, :, :], per_node(degree), ALU.mult))
                link(dve, dve.tensor_copy(cat[:, :, D:2 * D], h[:, :, :]))
        transpose_nodes(cat, 2 * D, hT[:, :])
        with nc.Block() as block:
            pe0, vec0 = at(s_pe), at(s_vec)
            cat_nodes = hT[:, :].rearrange("f (p t) -> f t p", t=NT)
            starts = list(range(0, NT, 8))

            @block.tensor
            def _(pe):
                for n, t0 in enumerate(starts):
                    if n >= 2:
                        pe.wait_ge(s_vec, vec0 + n - 1)
                    for t in range(t0, min(t0 + 8, NT)):
                        last = pe.matmul(banks[n % 2][:, (t - t0) * D:(t - t0 + 1) * D], cat_nodes[:, t, :],
                                         wv_sb[:, :], start=True, stop=True)
                    bump(s_pe, last)

            @block.vector
            def _(dve):
                for n, t0 in enumerate(starts):
                    dve.wait_ge(s_pe, pe0 + n + 1)
                    k = min(8, NT - t0)
                    bump(s_vec, dve.tensor_tensor(
                        tmp[:, t0:t0 + k, :], banks[n % 2][:, 0:k * D].rearrange("p (t f) -> p t f", f=D),
                        bv_sb[:, :].rearrange("p (o f) -> p o f", o=1).to_broadcast([P, k, D]), ALU.add))
                dve.wait_ge(s_vec, at(s_vec))
                link(dve, dve.scalar_tensor_tensor(x[:, :, :], tmp[:, :, :], 0.0, x[:, :, :], ALU.max, ALU.add))

        layernorm_relu()
        neighbours = sum_neighbours(h_rows[2], sums[2])
        with nc.Block() as block:
            @block.vector
            def _(dve):
                link(dve, dve.tensor_tensor(x[:, :, :], x[:, :, :], neighbours, ALU.add))
                counts["x"] = at(s_vec)

            @block.sync
            def _(sp):
                sp.wait_ge(s_vec, counts["x"])
                bump(s_store, sp.dma_start(out.rearrange("(p t) f -> p t f", t=NT), x[:, :, :]), 16)
                sp.wait_ge(s_store, at(s_store))


def kernel(**inputs):
    import concourse.bacc as bacc
    from concourse.bass_utils import run_bass_kernel_spmd

    arrays = lay_out(inputs)
    nc = bacc.Bacc("TRN2", target_bir_lowering=False, num_devices=1)
    args = [nc.dram_tensor(name, a.shape, mybir.dt.from_np(a.dtype), kind="ExternalInput").ap()
            for name, a in arrays.items()]
    out = nc.dram_tensor("out", (NPAD, D), F32, kind="ExternalOutput").ap()
    gnn_layers(nc, *args, out)
    r = run_bass_kernel_spmd(nc, [arrays], core_ids=[0])
    return r.results[0]["out"][0:N]


def lay_out(inputs):
    a = {k: np.ascontiguousarray(v) for k, v in inputs.items()}
    pad = T * P - E

    def edges(v, fill=0):
        return np.concatenate([v, np.full((pad, *v.shape[1:]), fill, v.dtype)])

    dst = edges(a["dst"].astype(np.int32), NO_NODE)
    arrays = {
        "x_in": np.concatenate([a["x"], np.zeros((NPAD - N, D), np.float32)]),
        "src_c": edges(a["src"].astype(np.int32)).reshape(T, P).T,
        "dst_c": dst.reshape(T, P).T,
        "dst_r": dst.reshape(C, EC),
        "ea32_t": edges(a["edge_attr_32"]).T,
        "ea64_c": edges(a["edge_attr_64"]).reshape(C, G, P, D).transpose(0, 2, 1, 3),
        "beta": a["L0_gnn_beta"], "eps": a["L1_gnn_eps"],
        "w1": a["L1_gnn_W1"], "b1": a["L1_gnn_b1"], "gamma1": a["L1_gnn_gamma1"], "beta1": a["L1_gnn_beta1"],
        "w2": a["L1_gnn_W2"], "b2": a["L1_gnn_b2"], "gamma2": a["L1_gnn_gamma2"], "beta2": a["L1_gnn_beta2"],
        "w_e": a["L2_gnn_W_e"], "b_e": a["L2_gnn_b_e"], "w_v": a["L2_gnn_W_v"], "b_v": a["L2_gnn_b_v"],
    }
    return {k: np.ascontiguousarray(v) for k, v in arrays.items()}
```

```python
import numpy as np
import concourse.bass as bass
from concourse import mybir
from contextlib import ExitStack

F32 = mybir.dt.float32
I32 = mybir.dt.int32
I16 = mybir.dt.int16
F16 = mybir.dt.float16
ALU = mybir.AluOpType
ACT = mybir.ActivationFunctionType
AX = mybir.AxisListType

N, E, D = 6250, 206250, 64
D_EDGE = 32
P = 128
NT = -(-N // P)
NPAD = P * NT
NROWS = NPAD + P
G = 14
C = -(-E // (P * G))
PART = 8
NS = 4
GROUPS = C // NS
T = C * G
EC = G * P
W = 64
NO_NODE = 16384
MAX_PASSES = N // W + 1
BIG = 1.0e30
LN_EPS = BN_EPS = 1e-5
ROW0 = D + 2
ST0 = 2 * D + 3
S_DEN, S_MAX, S_EA, S_DEG = D, D + 1, D + 2, 2 * D + 2
NQ = -(-NPAD // 512)
PAIRS = T // 2
CP = G // 2
PW = 12
PH = PW // 2
CR = 4
CU = 4
CW = W + PW
NB = 224
SPLIT = 2.0 ** 11
assert C % NS == 0 and NS % 2 == 0 and N + W <= NROWS and G % 2 == 0 and NPAD % (2 * NB) == 0
assert PART < G
assert C % CU == 0 and CU * CP % CR == 0 and CU % 2 == 0


def gnn_layers(nc, x_in, src_c, dst_c, dst_r, ea32_t, ea64_c, beta, eps, w1, b1, gamma1, beta1,
               w2, b2, gamma2, beta2, w_e, b_e, w_v, b_v, out):
    ctx = ExitStack()
    with ctx:
        def sb(name, shape, dt=F32):
            return ctx.enter_context(nc.sbuf_tensor(name, shape, dt))

        def ps(name, shape):
            return ctx.enter_context(nc.psum_tensor(name, shape, F32))

        def sem(name):
            return ctx.enter_context(nc.semaphore(name))

        def dram(name, shape, dt=F32):
            return nc.dram_tensor(name, shape, dt, kind="Internal").ap()

        h0_rows = dram("h0_rows", (NPAD, ROW0))
        h_rows = [dram(f"h_rows{i}", (NPAD, D)) for i in range(3)]
        win_rows = [dram(f"win_rows{i}", (NROWS, D)) for i in range(2)]
        state0 = dram("state0", (NROWS, ST0))
        sums = [dram(f"sums{i}", (NROWS, D)) for i in range(3)]
        span_d = dram("span_d", (C, 2))
        rel_rows = dram("rel_rows", (C, EC), I16)
        pair_d = dram("pair_d", (2, PAIRS))
        edge_counts = dram("edge_counts", (P, NROWS * NT), F16)

        x = sb("x", [P, NT, D])
        h = sb("h", [P, NT, D])
        h_flat = h[:, :, :].rearrange("p t f -> p (t f)")
        tmp = sb("tmp", [P, NT, D])
        arena = sb("arena", [P, NT * ST0])
        state = arena[:, :].rearrange("p (t f) -> p t f", f=ST0)
        cat = arena[:, 0:NT * 2 * D].rearrange("p (t f) -> p t f", f=2 * D)
        y1t = arena[:, 0:NPAD]
        hT = sb("hT", [P, NPAD])
        ident = sb("ident", [P, P])
        halves = sb("halves", [P, D])
        dense = sb("dense", [1, 1], I32)
        tests = sb("tests", [1, 8])
        col = sb("col", [P, 8, NT])
        w1_sb = sb("w1_sb", [D, 2 * D])
        w2_sb = sb("w2_sb", [2 * D, D])
        wsd_sb = sb("wsd_sb", [D + 1, 2 * D])
        wv_sb = sb("wv_sb", [2 * D, D])
        bv_sb = sb("bv_sb", [P, D])
        par = sb("par", [P, 8])
        bn1 = sb("bn1", [P, NQ, 6])
        bna = sb("bna", [P, 8])
        src_sb = sb("src_sb", [P, T + (NS - 1) * G], I32)
        dcol = sb("dcol", [P, T])
        iota_row = sb("iota_row", [P, 2, W])
        iota_col = sb("iota_col", [P, 2])
        base0 = sb("base0", [1, C], I32)
        base = sb("base", [1, C], I32)
        spans = sb("spans", [P, C, 2])
        stat = sb("stat", [P, 8])
        pair_stat = sb("pair_stat", [P, 2 * CP])
        passes = sb("passes", [1, 2], I32)
        idx = sb("idx", [P, NS, G], I32)
        g = sb("g", [P, NS, G, ROW0])
        onehot = sb("onehot", [P, 2, G, W])
        weighted = sb("weighted", [P, G, W])
        product = sb("product", [P, G, W])
        hot_src = sb("hot_src", [P, CU, P, G], F16)
        edge_space = sb("edge_space", [P, 4 * EC])
        lhs = edge_space[0:W + D_EDGE, 0:2 * EC].rearrange("w (s e) -> w s e", s=2)
        off_window = edge_space[0:W, 2 * EC:4 * EC].rearrange("w (s e) -> w s e", s=2)
        drow = sb("drow", [W, 2, EC], I16)
        ea = sb("ea", [P, 2, G, D + 1])
        win = sb("win", [W + D_EDGE, 2, D])
        sc = sb("sc", [P, 2, 4, G])
        st_in = sb("st_in", [W, ST0])
        st_out = sb("st_out", [W, ST0])
        mrg = sb("mrg", [W, 2, 8])
        rel16 = weighted[:, :, :].rearrange("p g w -> p (g w)").bitcast(I16)[:, 0:EC]
        key, key_next, src_row = hT[:, 0:T], hT[:, T:2 * T], hT[:, 2 * T:3 * T]
        pair_min, pair_max = h_flat[:, 0:PAIRS + 2], h_flat[0:1, PAIRS + 2:2 * PAIRS + 2]
        offset = h_flat[0:1, 2 * PAIRS + 2:3 * PAIRS + 2].bitcast(I32)
        quotient, dst, place = (edge_space[:, i * T:(i + 1) * T] for i in range(3))
        iota_wide, offset_f = edge_space[:, 3 * T:3 * T + PW * NT], edge_space[0:1, 3 * T + 600:3 * T + 600 + PAIRS]
        one16 = tmp[:, :, :].rearrange("p t f -> p (t f)").bitcast(F16)
        iota16 = one16[:, 0:PW * NT]
        hot_dst = one16[:, 600:600 + 2 * CR * PW * NT].rearrange("p (s n) -> p s n", s=2 * CR)
        iota_tiles = edge_space[:, 0:P * G // 2].bitcast(F16).rearrange("p (n g) -> p n g", g=G)
        hot_next = edge_space[:, 3000:3000 + CU * NT * G // 2].bitcast(F16) \
            .rearrange("p (s n g) -> p s n g", s=CU, g=G)
        src_row16 = hT[:, 3 * T:3 * T + PAIRS + 2 * CP].bitcast(F16)
        key_next16 = edge_space[:, 6300:6300 + PAIRS + 2 * CP].bitcast(F16)
        chunk_counts = [space.bitcast(F16) for space in
                        [arena[:, i * 1920:i * 1920 + CW * NT // 2] for i in range(CU - 1)]
                        + [edge_space[:, 1000:1000 + CW * NT // 2]]]
        parts = g[:, :, :, :].rearrange("p s g f -> p (s g f)").bitcast(F16)[:, 0:NT * 2 * D] \
            .rearrange("p (t f) -> p t f", f=2 * D)
        blocks = [space.bitcast(F16).rearrange("p (w a) -> p w a", a=NT)
                  for space in (arena[:, 0:NB * NT // 2], edge_space[:, 0:NB * NT // 2])]
        ps_x = ps("ps_x", [P, 16, W])
        ps_t = ps("ps_t", [P, 16, P])
        ps_ab = ps("ps_ab", [P, 2, 512])
        ps_a, ps_b = ps_ab[:, 0, :], ps_ab[:, 1, :]
        turned = ps_t[:, :, :].rearrange("p a b -> p (a b)")[:, 0:G * W].rearrange("p (g w) -> p g w", w=W)
        pair_banks = [ps_t[:, 0:8, :].rearrange("p (b x) c -> p b (x c)", b=2),
                      ps_t[:, 8:16, :].rearrange("p (b x) c -> p b (x c)", b=2),
                      ps_x[:, :, :].rearrange("p (b x) c -> p b (x c)", b=2), ps_ab[:, :, :]]
        banks = [ps_t[:, 4 * i:4 * i + 4, :].rearrange("p a b -> p (a b)") for i in range(4)]

        def iota_rows():
            return iota_row[:, 1, :].rearrange("p (o w) -> p o w", o=1).to_broadcast([P, G, W])

        def per_edge(a):
            return a.rearrange("p (g o) -> p g o", o=1).to_broadcast([P, G, W])

        def per_node(a):
            return a.rearrange("p (t o) -> p t o", o=1).to_broadcast([P, NT, D])

        def node_rows(table, width):
            return table[0:NPAD, 0:width].rearrange("(p t) f -> p t f", t=NT)

        s_load = sem("s_load")
        s_vec = sem("s_vec")
        s_act = sem("s_act")
        s_pool = sem("s_pool")
        s_pe = sem("s_pe")
        s_store = sem("s_store")
        s_spans = sem("s_spans")
        s_pairs = sem("s_pairs")
        s_tail = sem("s_tail")
        c_made, c_counted, c_copied = sem("c_made"), sem("c_counted"), sem("c_copied")
        c_stored = sem("c_stored")
        d_loaded = [sem("d_loaded0"), sem("d_loaded1")]
        d_split, d_parts, d_product, d_copied = sem("d_split"), sem("d_parts"), sem("d_product"), sem("d_copied")
        d_rows, d_added = sem("d_rows"), sem("d_added")
        d_fetched, d_gathered = sem("d_fetched"), sem("d_gathered")

        counts = {}

        def bump(which, ins, by=1):
            ins.then_inc(which, by)
            counts[which.name] = counts.get(which.name, 0) + by
            return counts.get(which.name, 0)

        def at(which):
            return counts.get(which.name, 0)

        def link(eng, ins):
            eng.wait_ge(s_vec, bump(s_vec, ins))

        with nc.Block() as block:
            @block.sync
            def _(sp):
                def load(dst, src):
                    bump(s_load, sp.dma_start(dst, src), 16)

                load(x[:, :, :], x_in.rearrange("(p t) f -> p t f", t=NT))
                load(src_sb[:, 0:T], src_c)
                load(arena[:, 0:T].bitcast(I32), dst_c)
                load(hT[0:C, 0:EC].bitcast(I32), dst_r)
                with nc.allow_non_contiguous_dma("a value per partition"):
                    load(par[:, 0:1], b1.rearrange("(p o) -> p o", o=1))
                    load(par[:, 1:2], gamma1.rearrange("(p o) -> p o", o=1))
                    load(par[:, 2:3], beta1.rearrange("(p o) -> p o", o=1))
                    load(par[0:D, 3:4], b2.rearrange("(p o) -> p o", o=1))
                    load(par[0:D, 4:5], gamma2.rearrange("(p o) -> p o", o=1))
                    load(par[0:D, 5:6], beta2.rearrange("(p o) -> p o", o=1))
                    load(par[:, 6:7], beta.rearrange("(p o) -> p o", o=1).to_broadcast([P, 1]))
                    load(par[:, 7:8], eps.rearrange("(p o) -> p o", o=1).to_broadcast([P, 1]))
                load(w1_sb[:, :], w1)
                load(w2_sb[:, :], w2)
                load(wsd_sb[0:D, 0:D], w_e[0:D, :])
                load(wsd_sb[0:D, D:2 * D], w_e[D + D_EDGE:2 * D + D_EDGE, :])
                load(wsd_sb[D:D + 1, D:2 * D], b_e.rearrange("(o f) -> o f", o=1))
                for j in range(2):
                    load(win[W:W + D_EDGE, j, :], w_e[D:D + D_EDGE, :])
                load(wv_sb[:, :], w_v)
                load(bv_sb[:, :], b_v.rearrange("(o f) -> o f", o=1).to_broadcast([P, D]))

            @block.gpsimd
            def _(pool):
                pool.memset(ident[:, :], 0.0).then_inc(s_pool, 1)
                pool.wait_ge(s_pool, 1)
                pool.affine_select(out=ident[:, :], in_=ident[:, :], compare_op=ALU.not_equal, fill=1.0,
                                   base=0, pattern=[[-1, P]], channel_multiplier=1).then_inc(s_pool, 1)
                pool.iota(iota_row[:, 0, :], pattern=[[1, W]], base=0, channel_multiplier=0,
                          allow_small_or_imprecise_dtypes=True).then_inc(s_pool, 1)
                pool.iota(iota_col[:, 0:1], pattern=[[0, 1]], base=0, channel_multiplier=1,
                          allow_small_or_imprecise_dtypes=True).then_inc(s_pool, 1)
                pool.wait_ge(s_pool, 4)

            @block.vector
            def _(dve):
                dve.memset(ea[:, :, :, D:D + 1], 1.0)
                dve.memset(wsd_sb[D:D + 1, 0:D], 0.0)
                dve.memset(src_sb[:, T:T + (NS - 1) * G], 0)
                link(dve, dve.memset(tmp[:, :, :], 0.0))
                dve.wait_ge(s_load, at(s_load))

        with nc.Block() as block:
            @block.vector
            def _(dve):
                dst, dstf, real = hT[0:C, 0:EC].bitcast(I32), hT[0:C, 2048:2048 + EC], hT[0:C, 4096:4096 + EC]
                link(dve, dve.tensor_copy(dstf, dst))
                link(dve, dve.tensor_reduce(stat[0:C, 0:1], dstf, AX.X, ALU.min))
                link(dve, dve.tensor_scalar(real, dstf, float(N), None, ALU.is_lt))
                link(dve, dve.tensor_tensor(real, dstf, real, ALU.mult))
                link(dve, dve.tensor_reduce(stat[0:C, 2:3], real, AX.X, ALU.max))
                link(dve, dve.tensor_tensor(stat[0:C, 1:2], stat[0:C, 2:3], stat[0:C, 0:1], ALU.subtract))
                counts["spans known"] = at(s_vec)
                link(dve, dve.tensor_scalar(rel16[0:C, :], dstf, stat[0:C, 0:1], None, ALU.subtract))
                counts["rows relative"] = at(s_vec)
                pairs = [v.rearrange("c (q e) -> c q e", q=CP) for v in (dstf, real)]
                link(dve, dve.tensor_reduce(pair_stat[0:C, 0:CP], pairs[0], AX.X, ALU.min))
                link(dve, dve.tensor_scalar(pair_stat[0:C, 0:CP], pair_stat[0:C, 0:CP], float(N), None, ALU.min))
                link(dve, dve.tensor_reduce(pair_stat[0:C, CP:2 * CP], pairs[1], AX.X, ALU.max))
                counts["pairs known"] = at(s_vec)
                dve.wait_ge(s_spans, 16)
                link(dve, dve.tensor_copy(base0[0:1, :], spans[0:1, :, 0]))
                link(dve, dve.tensor_reduce(stat[0:1, 4:5], spans[0:1, :, 1], AX.X, ALU.max))
                link(dve, dve.tensor_copy(passes[0:1, 0:1], stat[0:1, 4:5]))
                link(dve, dve.tensor_scalar(passes[0:1, 0:1], passes[0:1, 0:1], W.bit_length() - 1, None,
                                            ALU.arith_shift_right))
                link(dve, dve.tensor_scalar(passes[0:1, 1:2], passes[0:1, 0:1], 1.0, None, ALU.add))
                link(dve, dve.tensor_copy(dcol[:, 0:T], arena[:, 0:T].bitcast(I32)))
                link(dve, dve.tensor_tensor(
                    dcol[:, 0:T].rearrange("p (c g) -> p c g", g=G),
                    dcol[:, 0:T].rearrange("p (c g) -> p c g", g=G),
                    spans[:, :, 0:1].to_broadcast([P, C, G]), ALU.subtract))

            @block.sync
            def _(sp):
                sp.wait_ge(s_vec, counts["spans known"])
                sp.dma_start(span_d, stat[0:C, 0:2]).then_inc(s_store, 16)
                sp.wait_ge(s_store, 16)
                sp.dma_start(spans[:, :, :], span_d.rearrange("(o c) f -> o c f", o=1)
                             .to_broadcast([P, C, 2])).then_inc(s_spans, 16)
                sp.wait_ge(s_vec, counts["rows relative"])
                sp.dma_start(rel_rows[0:C, :], rel16[0:C, :]).then_inc(s_store, 16)
                sp.wait_ge(s_vec, counts["pairs known"])
                for i in range(2):
                    sp.dma_start(pair_d[i:i + 1, :].rearrange("o (c q) -> (o c) q", q=CP),
                                 pair_stat[0:C, i * CP:(i + 1) * CP]).then_inc(s_store, 16)
                sp.wait_ge(s_store, 64)
                counts[s_store.name] = 64
                sp.dma_start(pair_min[:, 0:PAIRS], pair_d[0:1, :].to_broadcast([P, PAIRS])).then_inc(s_pairs, 16)
                sp.dma_start(pair_max, pair_d[1:2, :]).then_inc(s_pairs, 16)
                sp.wait_ge(s_pairs, 32)

        half = -(-NT // 2) + 3
        no_state = g[:, :, :, :].rearrange("p s g f -> p (s g f)")[:, 0:half * ST0] \
            .rearrange("p (t f) -> p t f", f=ST0)
        no_rows = onehot[:, :, :, :].rearrange("p s g w -> p (s g) w")[:, 0:half, :]
        with nc.Block() as block:
            @block.vector
            def _(dve):
                dve.memset(no_rows, 0.0)
                link(dve, dve.memset(no_state, 0.0))
                link(dve, dve.memset(no_state[:, :, S_MAX:S_MAX + 1], -BIG))
                counts["zeroed"] = at(s_vec)

            @block.sync
            def _(sp):
                def clear(table, width, rows):
                    for t0, t1 in ((0, half), (half, NT)):
                        bump(s_store, sp.dma_start(node_rows(table, width)[:, t0:t1, :],
                                                   rows[:, 0:t1 - t0, :]), 16)
                    bump(s_store, sp.dma_start(table[NPAD:NROWS, :], rows[:, 0, :]), 16)

                sp.wait_ge(s_vec, counts["zeroed"])
                sp.dma_start(edge_counts[:, N * NT:NPAD * NT],
                             onehot[:, :, :, :].rearrange("p s g w -> p (s g w)").bitcast(F16)
                             [:, 0:(NPAD - N) * NT]).then_inc(s_tail, 16)
                clear(state0, ST0, no_state)
                for table in sums:
                    clear(table, D, no_rows)
                for table in win_rows:
                    bump(s_store, sp.dma_start(table[NPAD:NROWS, :], no_rows[:, 0, :]), 16)
                sp.wait_ge(s_tail, 16)

        def layernorm_relu():
            mean, var = col[:, 0, :], col[:, 1, :]
            squares = hT[:, 0:NT * D].rearrange("p (t f) -> p t f", f=D)
            with nc.Block() as block:
                @block.vector
                def _(dve):
                    link(dve, dve.tensor_reduce(mean, x[:, :, :], AX.X, ALU.add))
                    link(dve, dve.tensor_scalar(mean, mean, 1.0 / D, None, ALU.mult))
                    link(dve, dve.tensor_tensor(h[:, :, :], x[:, :, :], per_node(mean), ALU.subtract))
                    link(dve, dve.tensor_tensor(squares, h[:, :, :], h[:, :, :], ALU.mult))
                    link(dve, dve.tensor_reduce(var, squares, AX.X, ALU.add))
                    link(dve, dve.tensor_scalar(var, var, 1.0 / D, LN_EPS, ALU.mult, ALU.add))
                    counts["variance"] = at(s_vec)
                    dve.wait_ge(s_act, at(s_act) + 1)
                    link(dve, dve.reciprocal(var, var))
                    link(dve, dve.scalar_tensor_tensor(h[:, :, :], h[:, :, :], 0.0, per_node(var),
                                                       ALU.max, ALU.mult))

                @block.scalar
                def _(act):
                    act.wait_ge(s_vec, counts["variance"])
                    bump(s_act, act.activation(var, var, ACT.Sqrt))

        def transpose_nodes(rows, width, to):
            first, done = at(s_pe), at(s_vec)
            by_node = to.rearrange("f (p t) -> f t p", t=NT)
            starts = list(range(0, NT, 4))
            with nc.Block() as block:
                @block.tensor
                def _(pe):
                    for n, t0 in enumerate(starts):
                        if n >= 2:
                            pe.wait_ge(s_vec, done + n - 1)
                        for t in range(t0, min(t0 + 4, NT)):
                            last = pe.transpose(banks[n % 2][0:width, (t - t0) * P:(t - t0 + 1) * P],
                                                rows[:, t, :], ident[:, :])
                        bump(s_pe, last)

                @block.vector
                def _(dve):
                    for n, t0 in enumerate(starts):
                        dve.wait_ge(s_pe, first + n + 1)
                        k = min(4, NT - t0)
                        bump(s_vec, dve.tensor_copy(
                            by_node[:, t0:t0 + k, :],
                            banks[n % 2][0:width, 0:k * P].rearrange("f (t p) -> f t p", t=k)))
                    dve.wait_ge(s_vec, at(s_vec))

        def project(weights, rows_in, to, bias, gamma, shift, width, stats):
            pe0, act0 = at(s_pe), at(s_act)
            mv, scale = bna[0:width, 0:2], bna[0:width, 2:3]
            with nc.Block() as block:
                @block.tensor
                def _(pe):
                    for q in range(NQ):
                        n = min(512, NPAD - 512 * q)
                        if q >= 2:
                            pe.wait_ge(s_act, act0 + q - 1)
                        bump(s_pe, pe.matmul(banks[q % 2][0:width, 0:n], weights,
                                             rows_in[:, 512 * q:512 * q + n], start=True, stop=True))

                @block.scalar
                def _(act):
                    for q in range(NQ):
                        n = min(512, NPAD - 512 * q)
                        act.wait_ge(s_pe, pe0 + q + 1)
                        bump(s_act, act.activation(to[:, 512 * q:512 * q + n], banks[q % 2][0:width, 0:n],
                                                   ACT.Identity, bias=bias))

                @block.vector
                def _(dve):
                    for q in range(NQ):
                        n = min(512, N - 512 * q)
                        dve.wait_ge(s_act, act0 + q + 1)
                        link(dve, dve.bn_stats(stats[0:width, q, :], to[:, 512 * q:512 * q + n]))
                    link(dve, dve.bn_aggr(mv, stats[0:width, :, :].rearrange("p q s -> p (q s)")))
                    link(dve, dve.tensor_scalar(scale, mv[:, 1:2], BN_EPS, None, ALU.add))
                    counts["variance"] = at(s_vec)

            with nc.Block() as block:
                @block.vector
                def _(dve):
                    dve.wait_ge(s_act, at(s_act) + 1)
                    link(dve, dve.reciprocal(scale, scale))
                    link(dve, dve.tensor_tensor(scale, scale, gamma, ALU.mult))
                    link(dve, dve.tensor_tensor(bna[0:width, 3:4], mv[:, 0:1], scale, ALU.mult))
                    link(dve, dve.tensor_tensor(bna[0:width, 4:5], shift, bna[0:width, 3:4], ALU.subtract))
                    counts["affine"] = at(s_vec)

                @block.scalar
                def _(act):
                    bump(s_act, act.activation(scale, scale, ACT.Sqrt))
                    act.wait_ge(s_vec, counts["affine"])
                    bump(s_act, act.activation(to, to, ACT.Relu, scale=scale, bias=bna[0:width, 4:5]))
                    act.wait_ge(s_act, at(s_act))

        def store_rows(pairs):
            with nc.Block() as block:
                @block.sync
                def _(sp):
                    for table, rows in pairs:
                        bump(s_store, sp.dma_start(table, rows), 16)
                    sp.wait_ge(s_store, at(s_store))

        def load_rows(rows, table):
            with nc.Block() as block:
                @block.sync
                def _(sp):
                    bump(s_load, sp.dma_start(rows, table), 16)
                    sp.wait_ge(s_load, at(s_load))

        e = {name: sem("e_" + name) for name in (
            "idx", "gathering", "rows0", "rows1", "rows2", "rows3", "loading", "rel0", "rel1", "attr0", "attr1",
            "win0", "win1", "hot", "columns", "dst", "product", "dot", "score", "spreading", "spread",
            "reducing", "part_top", "top", "minus_top", "p", "turning", "turned", "weighted", "summed", "attr_summed",
            "state", "new_top", "pair", "scales", "scaled", "merged", "stored")}
        START = {"hot": 2, "dst": 2, "summed": 4, "attr_summed": 2, "turned": 2, "weighted": 1,
                 "merged": 1, "score": 1, "product": 1}

        def done(name, k):
            return k + 1 + START.get(name, 0)

        def start_counts(eng, *names):
            for name in names:
                eng.sem_inc(e[name], START[name])

        def start_windows():
            with nc.Block() as block:
                @block.vector
                def _(dve):
                    bump(s_vec, dve.tensor_copy(base[:, :], base0[:, :]))
                    bump(s_vec, dve.tensor_copy(iota_row[:, 1, :], iota_row[:, 0, :]))
                    link(dve, dve.tensor_copy(iota_col[:, 1:2], iota_col[:, 0:1]))

        def next_windows():
            with nc.Block() as block:
                @block.vector
                def _(dve):
                    dve.tensor_scalar(base[:, :], base[:, :], float(W), float(N), ALU.add, ALU.min)
                    dve.tensor_scalar(iota_row[:, 1, :], iota_row[:, 1, :], float(W), None, ALU.add)
                    dve.tensor_scalar(iota_col[:, 1:2], iota_col[:, 1:2], float(W), None, ALU.add)

        def over_windows(one_pass):
            start_windows()
            n = nc.values_load(passes[0:1, 1:2], min_val=1, max_val=MAX_PASSES)
            with nc.Fori(0, n):
                nc.gpsimd.dma_reset()
                nc.all_engine_barrier()
                for s in e.values():
                    nc.sync.sem_clear(s)
                nc.all_engine_barrier()
                one_pass()
                next_windows()

        def gather_chunks(pool, table, width):
            with pool.Fori(0, GROUPS) as i:
                for j in range(NS):
                    k = i * NS + j
                    pool.wait_ge(e["summed"], done("summed", k - NS))
                    pool.wait_ge(e["idx"], k + 1)
                    pool.sem_inc(e["gathering"], 1)
                    for t in range(G):
                        pool.indirect_dma_start(
                            g[:, j, t, 0:width], None, table,
                            bass.IndirectOffsetOnAxis(ap=idx[:, j, t:t + 1], axis=0)
                        ).then_inc(e[f"rows{j}"], 16)
            for j in range(NS):
                pool.wait_ge(e[f"rows{j}"], GROUPS * G * 16)

        def take_sources(dve, k, j):
            dve.wait_ge(e["summed"], done("summed", k - NS))
            dve.tensor_copy(idx[:, j, :], src_sb[:, bass.ds(k * G, G)]).then_inc(e["idx"], 1)

        def window_of(eng, k):
            return eng.value_load(base[0:1, bass.ds(k, 1)], min_val=0, max_val=N)

        def attention_pass():
            def loads(i, j):
                return i * (NS * 8) + j // 2 * 16 + 16

            def over_chunks(eng, step):
                with eng.Fori(0, GROUPS - 1) as i:
                    for j in range(NS):
                        step(i, j, True)
                for j in range(NS):
                    step(GROUPS - 1, j, j < NS - 1)

            with nc.Block() as block:
                @block.gpsimd
                def _(pool):
                    gather_chunks(pool, h0_rows, ROW0)

                @block.sync
                def _(sp):
                    def load_destinations(k, s):
                        sp.wait_ge(e["hot"], done("hot", k - 2))
                        sp.sem_inc(e["loading"], 1)
                        sp.dma_start(drow[:, s, :], rel_rows[bass.ds(k, 1), :]
                                     .to_broadcast([W, EC])).then_inc(e[f"rel{s}"], 16)

                    def load_window(k, s):
                        window = window_of(sp, k)
                        sp.wait_ge(e["dst"], done("dst", k - 2))
                        sp.sem_inc(e["loading"], 1)
                        sp.dma_start(win[0:W, s, :], win_rows[0][bass.ds(window, W), :]
                                     ).then_inc(e[f"win{s}"], 16)

                    def load_attributes(k, s):
                        sp.wait_ge(e["attr_summed"], done("attr_summed", k - 2))
                        sp.sem_inc(e["loading"], 1)
                        sp.dma_start(ea[:, s, :, 0:D], ea64_c[bass.ds(k, 1), :, :, :]
                                     .rearrange("o p g f -> (o p) g f")).then_inc(e[f"attr{s}"], 16)

                    def step(i, j, more):
                        k, s = i * NS + j, j % 2
                        rows = state0[bass.ds(window_of(sp, k), W), :]
                        sp.dma_start(st_in[:, :], rows).then_inc(e["state"], 16)
                        if not (type(i) is int and j >= NS - 3):
                            load_destinations(k + 3, 1 - s)
                            load_window(k + 3, 1 - s)
                        if not (type(i) is int and j >= NS - 2):
                            load_attributes(k + 2, s)
                        sp.wait_ge(e["merged"], done("merged", k))
                        sp.sem_inc(e["loading"], 1)
                        sp.dma_start(rows, st_out[:, :]).then_inc(e["stored"], 16)
                        sp.wait_ge(e["stored"], k * 16 + 16)
                        sp.sem_inc(e["loading"], 1)

                    for k in range(2):
                        load_destinations(k, k)
                        load_window(k, k)
                        load_attributes(k, k)
                    load_destinations(2, 0)
                    load_window(2, 0)
                    over_chunks(sp, step)

                @block.tensor
                def _(pe):
                    start_counts(pe, "dst", "summed", "attr_summed", "turned")

                    def spread_rows(i, j):
                        k, s = i * NS + j, j % 2
                        pe.wait_ge(e["hot"], done("hot", k))
                        pe.wait_ge(e[f"win{s}"], loads(i, j))
                        pe.wait_ge(e["product"], done("product", k - 1))
                        for t in range(G):
                            last = pe.matmul(ps_x[:, t, :], lhs[0:W, s, t * P:(t + 1) * P],
                                             win[0:W, s, :], start=True, stop=True)
                        last.then_inc(e["dst"], 1)

                    def spread_scores(i, j):
                        k, s = i * NS + j, j % 2
                        pe.wait_ge(e["weighted"], done("weighted", k - 1))
                        pe.wait_ge(e["score"], done("score", k))
                        pe.sem_inc(e["spreading"], 1)
                        for t in range(G):
                            last = pe.transpose(ps_t[0:W, t, :], sc[:, s, 0, t:t + 1].to_broadcast([P, W]),
                                                ident[:, :])
                            if t + 1 in (PART, G):
                                last.then_inc(e["spread"], 1)

                    def step(i, j, more):
                        k, s = i * NS + j, j % 2
                        for t in range(G):
                            if t in (0, PART):
                                pe.wait_ge(e["p"], k * 2 + (1 if t == 0 else 2))
                                pe.sem_inc(e["turning"], 1)
                            last = pe.transpose(turned[:, t, :], off_window[:, s, t * P:(t + 1) * P],
                                                ident[0:W, 0:W])
                        last.then_inc(e["turned"], 1)
                        if more:
                            spread_rows(i + (j + 1) // NS, (j + 1) % NS)
                        pe.wait_ge(e["merged"], done("merged", k - 1))
                        pe.wait_ge(e["weighted"], done("weighted", k))
                        for t in range(G):
                            last = pe.matmul(ps_a[0:W, 0:D + 1], weighted[:, t, :], g[:, j, t, 0:D + 1],
                                             start=(t == 0), stop=(t == G - 1))
                        last.then_inc(e["summed"], 1)
                        if more:
                            spread_scores(i + (j + 1) // NS, (j + 1) % NS)
                        pe.wait_ge(e["columns"], k + 1)
                        pe.wait_ge(e[f"attr{s}"], loads(i, j))
                        for t in range(G):
                            last = pe.matmul(ps_b[0:W, 0:D + 1], onehot[:, s, t, :], ea[:, s, t, :],
                                             start=(t == 0), stop=(t == G - 1))
                        last.then_inc(e["attr_summed"], 1)

                    spread_rows(0, 0)
                    spread_scores(0, 0)
                    over_chunks(pe, step)

                @block.vector
                def _(dve):
                    start_counts(dve, "hot", "merged", "score", "product")

                    def one_hots(i, j):
                        k, s = i * NS + j, j % 2
                        dve.wait_ge(e["turned"], done("turned", k - 2))
                        dve.wait_ge(e[f"rel{s}"], loads(i, j))
                        dve.tensor_scalar(lhs[0:W, s, :], drow[:, s, :], iota_col[0:W, 1:2], None,
                                          ALU.is_equal)
                        dve.tensor_scalar(off_window[:, s, :], drow[:, s, :], iota_col[0:W, 1:2], -2.0 * BIG,
                                          ALU.not_equal, ALU.mult).then_inc(e["hot"], 1)

                    def scores(i, j):
                        k, s = i * NS + j, j % 2
                        dve.wait_ge(e[f"rows{j}"], i * (16 * G) + 16 * G)
                        dve.wait_ge(e["dst"], done("dst", k))
                        dve.tensor_tensor(product[:, :, :], g[:, j, :, 0:D], ps_x[:, 0:G, :],
                                          ALU.mult).then_inc(e["product"], 1)
                        dve.wait_ge(e["product"], done("product", k))
                        dve.tensor_reduce(sc[:, s, 1, :], product[:, :, :], AX.X, ALU.add
                                          ).then_inc(e["dot"], 1)
                        dve.wait_ge(e["dot"], k + 1)
                        dve.scalar_tensor_tensor(sc[:, s, 0, :], sc[:, s, 1, :], par[:, 6:7],
                                                 g[:, j, :, D + 1], ALU.mult, ALU.mult
                                                 ).then_inc(e["score"], 1)

                    def maxima(i, j):
                        k, s = i * NS + j, j % 2
                        for n, (t0, t1) in enumerate(((0, PART), (PART, G))):
                            part = off_window[:, s, t0 * P:t1 * P].rearrange("w (g p) -> w g p", p=P)
                            dve.wait_ge(e["spread"], k * 2 + (n + 1))
                            if n == 1:
                                dve.wait_ge(e["part_top"], k + 1)
                            dve.sem_inc(e["reducing"], 1)
                            dve.tensor_tensor_reduce(
                                out=part, in0=ps_t[0:W, t0:t1, :], in1=part, scale=1.0,
                                scalar=-BIG if n == 0 else mrg[:, s, 7:8], op0=ALU.add, op1=ALU.max,
                                accum_out=mrg[:, s, 7:8] if n == 0 else mrg[:, s, 0:1]
                            ).then_inc(e["part_top"] if n == 0 else e["top"], 1)
                        dve.wait_ge(e["top"], k + 1)
                        dve.tensor_scalar(mrg[:, s, 6:7], mrg[:, s, 0:1], -1.0, None, ALU.mult
                                          ).then_inc(e["minus_top"], 1)

                    def step(i, j, more):
                        k, s = i * NS + j, j % 2
                        take_sources(dve, k + (NS - 1), (j + NS - 1) % NS)
                        dve.wait_ge(e["attr_summed"], done("attr_summed", k - 2))
                        dve.tensor_tensor(onehot[:, s, :, :], per_edge(dcol[:, bass.ds(k * G, G)]),
                                          iota_rows(), ALU.is_equal).then_inc(e["columns"], 1)
                        if more and not (type(i) is int and j == NS - 2):
                            one_hots(i + (j + 2) // NS, (j + 2) % NS)
                        if more:
                            scores(i + (j + 1) // NS, (j + 1) % NS)
                        dve.wait_ge(e["state"], k * 16 + 16)
                        dve.tensor_tensor(mrg[:, s, 1:2], mrg[:, s, 0:1], st_in[:, S_MAX:S_MAX + 1],
                                          ALU.max).then_inc(e["new_top"], 1)
                        dve.wait_ge(e["new_top"], k + 1)
                        dve.tensor_tensor(mrg[:, s, 2:3], st_in[:, S_MAX:S_MAX + 1], mrg[:, s, 1:2],
                                          ALU.subtract)
                        dve.tensor_tensor(mrg[:, s, 3:4], mrg[:, s, 0:1], mrg[:, s, 1:2],
                                          ALU.subtract).then_inc(e["pair"], 1)
                        dve.wait_ge(e["scales"], k + 1)
                        dve.tensor_scalar(st_out[:, 0:D + 1], st_in[:, 0:D + 1], mrg[:, s, 4:5], None,
                                          ALU.mult).then_inc(e["scaled"], 1)
                        dve.tensor_copy(st_out[:, S_MAX:S_MAX + 1], mrg[:, s, 1:2])
                        dve.wait_ge(e["summed"], done("summed", k))
                        dve.wait_ge(e["scaled"], k + 1)
                        dve.scalar_tensor_tensor(st_out[:, 0:D + 1], ps_a[0:W, 0:D + 1], mrg[:, s, 5:6],
                                                 st_out[:, 0:D + 1], ALU.mult, ALU.add)
                        if more:
                            maxima(i + (j + 1) // NS, (j + 1) % NS)
                        dve.wait_ge(e["attr_summed"], done("attr_summed", k))
                        dve.tensor_tensor(st_out[:, S_EA:ST0], st_in[:, S_EA:ST0],
                                          ps_b[0:W, 0:D + 1], ALU.add).then_inc(e["merged"], 1)

                    for k in range(NS - 1):
                        take_sources(dve, k, k)
                    one_hots(0, 0)
                    one_hots(0, 1)
                    scores(0, 0)
                    maxima(0, 0)
                    over_chunks(dve, step)

                @block.scalar
                def _(act):
                    start_counts(act, "weighted")
                    with act.Fori(0, GROUPS) as i:
                        for j in range(NS):
                            k, s = i * NS + j, j % 2
                            act.wait_ge(e["minus_top"], k + 1)
                            for t0, t1 in ((0, PART), (PART, G)):
                                part = off_window[:, s, t0 * P:t1 * P]
                                act.activation(part, part, ACT.Exp, bias=mrg[:, s, 6:7]).then_inc(e["p"], 1)
                            act.wait_ge(e["summed"], done("summed", k - 1))
                            act.wait_ge(e["turned"], done("turned", k))
                            act.activation(weighted[:, :, :], turned, ACT.Copy).then_inc(e["weighted"], 1)
                            act.wait_ge(e["pair"], k + 1)
                            act.activation(mrg[:, s, 4:6], mrg[:, s, 2:4], ACT.Exp).then_inc(e["scales"], 1)

        def is_dense(eng):
            return eng.value_load(dense[0:1, 0:1], min_val=0, max_val=1)

        def sum_pass(table, total):
            with nc.Block() as block:
                @block.gpsimd
                def _(pool):
                    with pool.If(is_dense(pool) == 0):
                        gather_chunks(pool, table, D)

                @block.tensor
                def _(pe):
                    with pe.If(is_dense(pe) == 0):
                        start_counts(pe, "summed")
                        with pe.Fori(0, GROUPS) as i:
                            for j in range(NS):
                                k = i * NS + j
                                pe.wait_ge(e["hot"], done("hot", k))
                                pe.wait_ge(e[f"rows{j}"], i * (16 * G) + 16 * G)
                                pe.wait_ge(e["merged"], done("merged", k - 1))
                                for t in range(G):
                                    last = pe.matmul(ps_a[0:W, 0:D], onehot[:, j % 2, t, :], g[:, j, t, 0:D],
                                                     start=(t == 0), stop=(t == G - 1))
                                last.then_inc(e["summed"], 1)

                @block.vector
                def _(dve):
                    with dve.If(is_dense(dve) == 0):
                        start_counts(dve, "hot", "merged")
                        for k in range(NS - 1):
                            take_sources(dve, k, k)
                        with dve.Fori(0, GROUPS) as i:
                            for j in range(NS):
                                k = i * NS + j
                                take_sources(dve, k + (NS - 1), (j + NS - 1) % NS)
                                dve.wait_ge(e["summed"], done("summed", k - 1))
                                dve.tensor_tensor(onehot[:, j % 2, :, :], per_edge(dcol[:, bass.ds(k * G, G)]),
                                                  iota_rows(), ALU.is_equal).then_inc(e["hot"], 1)
                                dve.wait_ge(e["state"], k * 16 + 16)
                                dve.wait_ge(e["summed"], done("summed", k))
                                dve.tensor_tensor(st_out[:, 0:D], st_in[:, 0:D], ps_a[0:W, 0:D],
                                                  ALU.add).then_inc(e["merged"], 1)

                @block.scalar
                def _(act):
                    with act.If(is_dense(act) == 0):
                        with act.Fori(0, GROUPS) as i:
                            for j in range(NS):
                                add_window(act, total, i * NS + j)

        def add_window(act, total, k):
            rows = total[bass.ds(window_of(act, k), W), :]
            act.dma_start(st_in[:, 0:D], rows).then_inc(e["state"], 16)
            act.wait_ge(e["merged"], done("merged", k))
            act.dma_start(rows, st_out[:, 0:D]).then_inc(e["stored"], 16)
            act.wait_ge(e["stored"], k * 16 + 16)

        def message_pass():
            with nc.Block() as block:
                @block.gpsimd
                def _(pool):
                    gather_chunks(pool, h_rows[1], D)

                @block.sync
                def _(sp):
                    with sp.Fori(0, GROUPS) as i:
                        for j in range(NS):
                            k = i * NS + j
                            window = window_of(sp, k)
                            sp.wait_ge(e["hot"], done("hot", k - 2))
                            sp.sem_inc(e["loading"], 1)
                            sp.dma_start(drow[:, j % 2, :], rel_rows[bass.ds(k, 1), :]
                                         .to_broadcast([W, EC])).then_inc(e[f"rel{j % 2}"], 16)
                            sp.wait_ge(e["dst"], done("dst", k - 2))
                            sp.sem_inc(e["loading"], 1)
                            sp.dma_start(lhs[W:W + D_EDGE, j % 2, :], ea32_t[:, bass.ds(k * EC, EC)]
                                         ).then_inc(e[f"attr{j % 2}"], 16)
                            sp.dma_start(win[0:W, j % 2, :], win_rows[1][bass.ds(window, W), :]
                                         ).then_inc(e[f"win{j % 2}"], 16)

                @block.tensor
                def _(pe):
                    start_counts(pe, "dst", "summed")
                    with pe.Fori(0, GROUPS) as i:
                        for j in range(NS):
                            k = i * NS + j
                            pe.wait_ge(e["hot"], done("hot", k))
                            pe.wait_ge(e[f"attr{j % 2}"], i * (NS * 8) + j // 2 * 16 + 16)
                            pe.wait_ge(e[f"win{j % 2}"], i * (NS * 8) + j // 2 * 16 + 16)
                            pe.wait_ge(e["score"], done("score", k - 1))
                            for t in range(G):
                                last = pe.matmul(ps_x[:, t, :], lhs[:, j % 2, t * P:(t + 1) * P],
                                                 win[:, j % 2, :], start=True, stop=True)
                            last.then_inc(e["dst"], 1)
                            pe.wait_ge(e["p"], k + 1)
                            pe.wait_ge(e["merged"], done("merged", k - 1))
                            for t in range(G):
                                last = pe.matmul(ps_a[0:W, 0:D], onehot[:, j % 2, t, :], weighted[:, t, :],
                                                 start=(t == 0), stop=(t == G - 1))
                            last.then_inc(e["summed"], 1)

                @block.vector
                def _(dve):
                    start_counts(dve, "hot", "merged", "score")
                    for k in range(NS - 1):
                        take_sources(dve, k, k)
                    with dve.Fori(0, GROUPS) as i:
                        for j in range(NS):
                            k = i * NS + j
                            take_sources(dve, k + (NS - 1), (j + NS - 1) % NS)
                            dve.wait_ge(e["summed"], done("summed", k - 1))
                            dve.tensor_tensor(onehot[:, j % 2, :, :], per_edge(dcol[:, bass.ds(k * G, G)]),
                                              iota_rows(), ALU.is_equal)
                            dve.wait_ge(e[f"rel{j % 2}"], i * (NS * 8) + j // 2 * 16 + 16)
                            dve.tensor_scalar(lhs[0:W, j % 2, :], drow[:, j % 2, :], iota_col[0:W, 1:2], None,
                                              ALU.is_equal).then_inc(e["hot"], 1)
                            dve.wait_ge(e[f"rows{j}"], i * (16 * G) + 16 * G)
                            dve.wait_ge(e["dst"], done("dst", k))
                            dve.tensor_tensor(weighted[:, :, :], g[:, j, :, 0:D], ps_x[:, 0:G, :],
                                              ALU.add).then_inc(e["score"], 1)
                            dve.wait_ge(e["state"], k * 16 + 16)
                            dve.wait_ge(e["summed"], done("summed", k))
                            dve.tensor_tensor(st_out[:, 0:D], st_in[:, 0:D], ps_a[0:W, 0:D],
                                              ALU.add).then_inc(e["merged"], 1)

                @block.scalar
                def _(act):
                    with act.Fori(0, GROUPS) as i:
                        for j in range(NS):
                            k = i * NS + j
                            rows = sums[1][bass.ds(window_of(act, k), W), :]
                            act.dma_start(st_in[:, 0:D], rows).then_inc(e["state"], 16)
                            act.wait_ge(e["score"], done("score", k))
                            act.activation(weighted[:, :, :], weighted[:, :, :], ACT.Relu
                                           ).then_inc(e["p"], 1)
                            act.wait_ge(e["merged"], done("merged", k))
                            act.dma_start(rows, st_out[:, 0:D]).then_inc(e["stored"], 16)
                            act.wait_ge(e["stored"], k * 16 + 16)

        def chunk_of(u):
            return u // (2 * CP) * 2 + u % 2

        def pair_of(u):
            return u % (2 * CP) // 2

        with nc.Block() as block:
            @block.gpsimd
            def _(pool):
                pool.iota(iota_wide, pattern=[[1, PW * NT]], base=0, channel_multiplier=0,
                          allow_small_or_imprecise_dtypes=True).then_inc(s_pool, 1)

            @block.vector
            def _(dve):
                first, second, third = pair_min[:, 0:PAIRS], pair_min[:, 1:PAIRS + 1], pair_min[:, 2:PAIRS + 2]
                link(dve, dve.memset(pair_min[:, PAIRS:PAIRS + 2], float(N)))

                def test(place, left, right, most):
                    n = left.shape[-1]
                    link(dve, dve.tensor_tensor(offset_f[:, 0:n], left, right, ALU.subtract))
                    link(dve, dve.tensor_reduce(tests[:, place:place + 1], offset_f[:, 0:n], AX.X, ALU.max))
                    link(dve, dve.tensor_scalar(tests[:, place:place + 1], tests[:, place:place + 1],
                                                float(most), None, ALU.subtract))

                test(0, second[0:1, :], first[0:1, :], PW)
                test(4, pair_min[0:1, CP:PAIRS + 1:CP], pair_min[0:1, 0:PAIRS:CP], W)
                test(1, pair_max, first[0:1, :], PW - 1)
                test(2, pair_max, second[0:1, :], 0)
                test(3, pair_max, third[0:1, :], -1)
                link(dve, dve.tensor_copy(tests[:, 5:6], first[0:1, 0:1]))
                link(dve, dve.tensor_reduce(tests[:, 6:7], tests[:, 0:6], AX.X, ALU.max))
                link(dve, dve.tensor_scalar(tests[:, 6:7], tests[:, 6:7], 0.0, None, ALU.is_le))
                link(dve, dve.tensor_copy(dense[:, :], tests[:, 6:7]))
                link(dve, dve.tensor_tensor(
                    offset_f.rearrange("o (c q) -> o c q", q=CP),
                    first[0:1, :].rearrange("o (c q) -> o c q", q=CP),
                    spans[0:1, :, 0:1].to_broadcast([1, C, CP]), ALU.subtract))
                link(dve, dve.tensor_scalar(offset_f, offset_f, 0.0, float(W), ALU.max, ALU.min))
                link(dve, dve.tensor_copy(offset, offset_f))
                whole = quotient.bitcast(I32)
                link(dve, dve.tensor_copy(key, src_sb[:, 0:T]))
                link(dve, dve.tensor_scalar(src_row, key, 1.0 / NT, None, ALU.mult))
                link(dve, dve.tensor_copy(whole, src_row))
                link(dve, dve.tensor_copy(src_row, whole))
                link(dve, dve.scalar_tensor_tensor(key, src_row, -float(NT), key, ALU.mult, ALU.add))
                for wrong, step in ((ALU.is_lt, -1.0), (ALU.is_ge, 1.0)):
                    link(dve, dve.tensor_scalar(key_next, key, 0.0 if step < 0 else float(NT), step,
                                                wrong, ALU.mult))
                    link(dve, dve.tensor_tensor(src_row, src_row, key_next, ALU.add))
                    link(dve, dve.scalar_tensor_tensor(key, key_next, -float(NT), key, ALU.mult, ALU.add))
                link(dve, dve.tensor_tensor(
                    dst.rearrange("p (c g) -> p c g", g=G), dcol[:, :].rearrange("p (c g) -> p c g", g=G),
                    spans[:, :, 0:1].to_broadcast([P, C, G]), ALU.add))
                for to, mins in ((key_next, second), (key, first)):
                    link(dve, dve.tensor_tensor(
                        place.rearrange("p (q s) -> p q s", s=2), dst.rearrange("p (q s) -> p q s", s=2),
                        mins.rearrange("p (q o) -> p q o", o=1).to_broadcast([P, PAIRS, 2]), ALU.subtract))
                    link(dve, dve.scalar_tensor_tensor(to, place, float(NT), key, ALU.mult, ALU.add))
                link(dve, dve.tensor_copy(src_row16[:, 0:T], src_row))
                link(dve, dve.tensor_scalar(key_next16[:, 0:T], key_next, 2000.0, -2000.0, ALU.min, ALU.max))
                dve.wait_ge(s_pool, 5)
                link(dve, dve.tensor_copy(iota16, iota_wide))
                link(dve, dve.scalar_tensor_tensor(halves[:, :], ident[:, D:2 * D], 1.0 / SPLIT, ident[:, 0:D],
                                                   ALU.mult, ALU.add))

        with nc.Block() as block:
            @block.vector
            def _(dve):
                link(dve, dve.memset(arena[:, 0:1920 * (CU - 1)], 0.0))
                link(dve, dve.memset(edge_space[:, 1000:6000], 0.0))
                link(dve, dve.tensor_copy(iota_tiles, iota16[:, 0:P].rearrange("p (n o) -> p n o", o=1)
                                          .to_broadcast([P, P, G])))
                link(dve, dve.memset(hot_src[:, CU - 1, :, :], 0.0))
                link(dve, dve.memset(src_row16[:, T:T + 2 * G], -1.0))
                link(dve, dve.memset(key_next16[:, T:T + 2 * G], -1.0))

        with nc.Block() as block:
            @block.vector
            def _(dve):
                def tile_hots(to, keys, first):
                    n = to.shape[1]
                    dve.tensor_tensor(to, iota_tiles[:, first:first + n, :],
                                      keys.rearrange("p (o g) -> p o g", o=1).to_broadcast([P, n, G]),
                                      ALU.is_equal)

                def source_hots(v, start, first):
                    tile_hots(hot_src[:, v, first:first + P // 2, :], src_row16[:, bass.ds(start, G)], first)

                def next_hots(v, start):
                    tile_hots(hot_next[:, v, :, :], key_next16[:, bass.ds(start, G)], 0)

                for v in range(2):
                    source_hots(v, v * G, 0)
                    source_hots(v, v * G, P // 2)
                    next_hots(v, v * G)
                with dve.Fori(0, C // CU) as i:
                    for u in range(CU * CP):
                        dve.wait_ge(c_counted, i * (CU * CP) + (u + 1))
                        if u % 2 == 1 and u % (2 * CP) > 2:
                            step, part = divmod((u % (2 * CP) - 3) // 2, 3)
                            ahead = u // (2 * CP) * 2 + 2 + step
                            start = (i * CU + ahead) * G
                            if part < 2:
                                source_hots(ahead % CU, start, part * (P // 2))
                            else:
                                next_hots(ahead % CU, start)
                        tile = i * (CU * G) + (chunk_of(u) * G + pair_of(u) * 2)
                        for s in range(2):
                            last = dve.tensor_scalar(hot_dst[:, 2 * (u % CR) + s, :], iota16,
                                                     key[:, bass.ds(tile + s, 1)], None, ALU.is_equal)
                        last.then_inc(c_made, 1)

            @block.tensor
            def _(pe):
                pe.sem_inc(c_counted, CR)
                with pe.Fori(0, C // CU) as i:
                    for u in range(CU * CP):
                        r, c, pair = i * (CU * CP) + u, chunk_of(u), pair_of(u)
                        to = pair_banks[u % CR]
                        pe.wait_ge(c_made, r + 1)
                        pe.wait_ge(c_copied, r + 1)
                        for s in range(2):
                            for b in range(2):
                                last = pe.matmul(to[:, b, 0:PH * NT], hot_src[:, c, :, 2 * pair + s],
                                                 hot_dst[:, 2 * (u % CR) + s, b * PH * NT:(b + 1) * PH * NT],
                                                 start=(s == 0), stop=(s == 1))
                            if s == 0:
                                before = (c * CP + pair - 1) % (CU * CP)
                                for t in range(2 * (before % CP), 2 * (before % CP) + 2):
                                    pe.matmul(to[:, 0, 0:NT], hot_src[:, before // CP, :, t],
                                              hot_next[:, before // CP, :, t], start=False, stop=False)
                        last.then_inc(c_counted, 1)

            @block.scalar
            def _(act):
                act.sem_inc(c_copied, CR)
                act.sem_inc(c_stored, 16 * CU)
                with act.Fori(0, C // CU) as i:
                    for u in range(CU * CP):
                        r, c, pair = i * (CU * CP) + u, chunk_of(u), pair_of(u)
                        if pair == 0:
                            act.wait_ge(c_stored, i * (CU * 16) + (c * 16 + 16))
                        start = act.value_load(offset[0:1, bass.ds(i * (CU * CP) + (c * CP + pair), 1)], min_val=0, max_val=W)
                        act.wait_ge(c_copied, r + (CR - 1))
                        act.wait_ge(c_counted, r + (CR + 1))
                        act.activation(
                            chunk_counts[c][:, bass.ds(start * NT, PW * NT)]
                            .rearrange("p (b n) -> p b n", b=2),
                            pair_banks[u % CR][:, :, 0:PH * NT], ACT.Copy).then_inc(c_copied, 1)

            @block.sync
            def _(sp):
                with sp.Fori(0, C // CU) as i:
                    for u in range(CU):
                        c = i * CU + u
                        window = sp.value_load(base0[0:1, bass.ds(c, 1)], min_val=0, max_val=N)
                        last = u // 2 * (2 * CP) + 2 * CP - 2 + u % 2
                        sp.wait_ge(c_copied, i * (CU * CP) + (last + 1 + CR))
                        sp.wait_ge(c_stored, c * 16 + 16 * CU)
                        sp.dma_start(edge_counts[:, bass.ds(window * NT, W * NT)],
                                     chunk_counts[u][:, 0:W * NT]).then_inc(c_stored, 16)
                sp.wait_ge(c_stored, C * 16 + 16 * CU)

        def load_first_counts():
            with nc.Block() as block:
                @block.sync
                def _(sp):
                    with sp.If(is_dense(sp) == 1):
                        for s in range(2):
                            sp.dma_start(blocks[s].rearrange("p w a -> p (w a)"),
                                         edge_counts[:, s * NB * NT:(s + 1) * NB * NT]
                                         ).then_inc(d_loaded[s], 16)

        def add_neighbours(to, table, total):
            blocks_done, rows_done, added_done = at(d_product), at(d_rows), at(d_added)
            copied0, parts0, split0 = at(d_copied), at(d_parts), at(d_split)
            loads0, fetched0 = at(d_loaded[0]), at(d_fetched)
            n_blocks = NPAD // NB
            sums_rows = arena[:, 0:NT * D].rearrange("p (t f) -> p t f", f=D)
            low = hT[:, 0:NT * D].rearrange("p (t f) -> p t f", f=D)
            by_node = hT[:, :].rearrange("f (p t) -> f t p", t=NT)
            starts = list(range(0, NT, 8))

            with nc.Block() as block:
                @block.sync
                def _(sp):
                    with sp.If(is_dense(sp) == 1):
                        with sp.Fori(0, n_blocks // 2 - 1) as i:
                            for s in range(2):
                                sp.wait_ge(d_product, i * 2 + (blocks_done + s + 1))
                                sp.sem_inc(d_fetched, 1)
                                sp.dma_start(blocks[s].rearrange("p w a -> p (w a)"),
                                             edge_counts[:, bass.ds(i * (2 * NB * NT) + (s + 2) * NB * NT,
                                                                    NB * NT)]
                                             ).then_inc(d_loaded[s], 16)

                @block.vector
                def _(dve):
                    with dve.If(is_dense(dve) == 1):
                        dve.tensor_copy(parts[:, :, 0:D], h[:, :, :]).then_inc(d_split, 1)
                        dve.wait_ge(d_split, split0 + 1)
                        dve.tensor_tensor(low, h[:, :, :], parts[:, :, 0:D], ALU.subtract).then_inc(d_split, 1)
                        dve.wait_ge(d_split, split0 + 2)
                        dve.tensor_scalar(parts[:, :, D:2 * D], low, SPLIT, None, ALU.mult).then_inc(d_split, 1)
                        dve.wait_ge(d_split, split0 + 3)
                        dve.sem_inc(d_parts, 1)
                        with dve.Fori(0, n_blocks // 2) as i:
                            for s in range(2):
                                dve.wait_ge(d_product, i * 2 + (blocks_done + s + 1))
                                dve.tensor_copy(hT[:, bass.ds(i * (2 * NB) + s * NB, NB)],
                                                banks[s][:, 0:NB]).then_inc(d_copied, 1)

                @block.tensor
                def _(pe):
                    with pe.If(is_dense(pe) == 1):
                        pe.wait_ge(d_parts, parts0 + 1)
                        with pe.Fori(0, n_blocks // 2) as i:
                            for s in range(2):
                                pe.wait_ge(d_loaded[s], i * 16 + (loads0 + 16))
                                pe.wait_ge(d_copied, i * 2 + (copied0 + s + 1))
                                for a in range(NT):
                                    last = pe.matmul(banks[s][:, 0:NB], parts[:, a, :], blocks[s][:, :, a],
                                                     start=(a == 0), stop=(a == NT - 1))
                                last.then_inc(d_product, 1)

                @block.scalar
                def _(act):
                    with act.If(is_dense(act) == 1):
                        act.sem_inc(d_copied, 2)
            for name, by in ((d_product, n_blocks), (d_copied, n_blocks + 2), (d_parts, 1), (d_split, 3),
                             (d_loaded[0], n_blocks // 2 * 16), (d_fetched, n_blocks - 2)):
                counts[name.name] = counts.get(name.name, 0) + by

            with nc.Block() as block:
                @block.tensor
                def _(pe):
                    with pe.If(is_dense(pe) == 1):
                        for n, t0 in enumerate(starts):
                            if n >= 2:
                                pe.wait_ge(d_added, added_done + n - 1)
                            for t in range(t0, min(t0 + 8, NT)):
                                last = pe.matmul(banks[n % 2][:, (t - t0) * D:(t - t0 + 1) * D],
                                                 by_node[:, t, :], halves[:, :], start=True, stop=True)
                            last.then_inc(d_rows, 1)

                @block.vector
                def _(dve):
                    with dve.If(is_dense(dve) == 1):
                        for n, t0 in enumerate(starts):
                            dve.wait_ge(d_rows, rows_done + n + 1)
                            k = min(8, NT - t0)
                            dve.tensor_tensor(
                                to[:, t0:t0 + k, :], to[:, t0:t0 + k, :],
                                banks[n % 2][:, 0:k * D].rearrange("p (t f) -> p t f", f=D), ALU.add
                            ).then_inc(d_added, 1)
                        dve.wait_ge(d_added, added_done + len(starts))

            for name in (d_rows, d_added):
                counts[name.name] = counts.get(name.name, 0) + len(starts)

            gathered0 = at(d_gathered)
            with nc.Block() as block:
                @block.sync
                def _(sp):
                    with sp.If(is_dense(sp) == 0):
                        sp.dma_start(node_rows(table, D), h[:, :, :]).then_inc(d_gathered, 16)
                        sp.wait_ge(d_gathered, gathered0 + 16)
            over_windows(lambda: sum_pass(table, total))
            with nc.Block() as block:
                @block.sync
                def _(sp):
                    with sp.If(is_dense(sp) == 0):
                        sp.dma_start(sums_rows, node_rows(total, D)).then_inc(d_gathered, 16)

                @block.vector
                def _(dve):
                    with dve.If(is_dense(dve) == 0):
                        dve.wait_ge(d_gathered, gathered0 + 32)
                        dve.tensor_tensor(to, to, sums_rows, ALU.add)
            counts[d_gathered.name] = gathered0 + 32

        layernorm_relu()
        norm, inv = col[:, 0, :], col[:, 1, :]
        with nc.Block() as block:
            @block.vector
            def _(dve):
                link(dve, dve.tensor_tensor(tmp[:, :, :], h[:, :, :], h[:, :, :], ALU.mult))
                link(dve, dve.tensor_reduce(norm, tmp[:, :, :], AX.X, ALU.add))
                counts["squares"] = at(s_vec)
                link(dve, dve.tensor_copy(state[:, :, 0:D], h[:, :, :]))
                link(dve, dve.memset(state[:, :, D:D + 1], 1.0))
                dve.wait_ge(s_act, at(s_act) + 1)
                link(dve, dve.tensor_scalar(norm, norm, 1e-12, None, ALU.max))
                link(dve, dve.reciprocal(inv, norm))
                link(dve, dve.tensor_copy(state[:, :, D + 1:D + 2], col[:, 1, :].rearrange("p (t o) -> p t o", o=1)))
                link(dve, dve.tensor_tensor(tmp[:, :, :], h[:, :, :], per_node(inv), ALU.mult))

            @block.scalar
            def _(act):
                act.wait_ge(s_vec, counts["squares"])
                bump(s_act, act.activation(norm, norm, ACT.Sqrt))

        store_rows([(node_rows(h0_rows, ROW0), state[:, :, 0:ROW0]), (node_rows(win_rows[0], D), tmp[:, :, :])])
        over_windows(attention_pass)
        load_rows(state, node_rows(state0, ST0))
        degree = col[:, 2, :]
        with nc.Block() as block:
            @block.vector
            def _(dve):
                link(dve, dve.tensor_scalar(norm, state[:, :, S_DEN], 1.2e-38, None, ALU.max))
                link(dve, dve.reciprocal(inv, norm))
                link(dve, dve.tensor_tensor(tmp[:, :, :], state[:, :, 0:D], per_node(inv), ALU.mult))
                link(dve, dve.tensor_tensor(x[:, :, :], x[:, :, :], tmp[:, :, :], ALU.add))
                link(dve, dve.tensor_scalar(degree, state[:, :, S_DEG], 1.0, None, ALU.max))
                link(dve, dve.reciprocal(degree, degree))
                link(dve, dve.tensor_copy(tmp[:, :, :], state[:, :, S_EA:S_EA + D]))

        load_first_counts()
        layernorm_relu()
        add_neighbours(tmp[:, :, :], h_rows[0], sums[0])
        with nc.Block() as block:
            @block.vector
            def _(dve):
                link(dve, dve.tensor_tensor(tmp[:, :, :], tmp[:, :, :], per_node(degree), ALU.mult))
                link(dve, dve.tensor_scalar(stat[:, 5:6], par[:, 7:8], 1.0, None, ALU.add))
                link(dve, dve.scalar_tensor_tensor(tmp[:, :, :], h[:, :, :], stat[:, 5:6], tmp[:, :, :],
                                                   ALU.mult, ALU.add))
        transpose_nodes(tmp, D, hT[0:D, :])
        project(w1_sb[:, :], hT[0:D, :], y1t, par[:, 0:1], par[:, 1:2], par[:, 2:3], P, bn1)
        project(w2_sb[:, :], y1t, hT[0:D, :], par[0:D, 3:4], par[0:D, 4:5], par[0:D, 5:6], D, bn1)
        with nc.Block() as block:
            pe0, vec0 = at(s_pe), at(s_vec)
            by_node = hT[0:D, :].rearrange("f (p t) -> f t p", t=NT)
            starts = list(range(0, NT, 8))

            @block.tensor
            def _(pe):
                for n, t0 in enumerate(starts):
                    if n >= 2:
                        pe.wait_ge(s_vec, vec0 + n - 1)
                    for t in range(t0, min(t0 + 8, NT)):
                        last = pe.transpose(banks[n % 2][:, (t - t0) * D:(t - t0 + 1) * D], by_node[:, t, :],
                                            ident[0:D, 0:D])
                    bump(s_pe, last)

            @block.vector
            def _(dve):
                for n, t0 in enumerate(starts):
                    dve.wait_ge(s_pe, pe0 + n + 1)
                    k = min(8, NT - t0)
                    bump(s_vec, dve.tensor_tensor(
                        x[:, t0:t0 + k, :], x[:, t0:t0 + k, :],
                        banks[n % 2][:, 0:k * D].rearrange("p (t f) -> p t f", f=D), ALU.add))
                dve.wait_ge(s_vec, at(s_vec))

        layernorm_relu()
        transpose_nodes(h, D, hT[0:D, :])
        with nc.Block() as block:
            pe0, vec0 = at(s_pe), at(s_vec)
            hT_nodes = hT[0:D + 1, :].rearrange("f (p t) -> f t p", t=NT)
            pq = arena[:, 0:NT * 2 * D].rearrange("p (t f) -> p t f", f=2 * D)
            starts = list(range(0, NT, 4))

            @block.tensor
            def _(pe):
                pe.wait_ge(s_vec, vec0 + 1)
                for n, t0 in enumerate(starts):
                    if n >= 2:
                        pe.wait_ge(s_vec, vec0 + n)
                    for t in range(t0, min(t0 + 4, NT)):
                        last = pe.matmul(banks[n % 2][:, (t - t0) * P:(t - t0 + 1) * P], hT_nodes[:, t, :],
                                         wsd_sb[:, :], start=True, stop=True)
                    bump(s_pe, last)

            @block.vector
            def _(dve):
                bump(s_vec, dve.memset(hT[D:D + 1, :], 1.0))
                for n, t0 in enumerate(starts):
                    dve.wait_ge(s_pe, pe0 + n + 1)
                    k = min(4, NT - t0)
                    bump(s_vec, dve.tensor_copy(
                        pq[:, t0:t0 + k, :], banks[n % 2][:, 0:k * P].rearrange("p (t f) -> p t f", f=P)))
                dve.wait_ge(s_vec, at(s_vec))

        store_rows([(node_rows(h_rows[1], D), pq[:, :, 0:D]), (node_rows(win_rows[1], D), pq[:, :, D:2 * D])])
        over_windows(message_pass)
        load_rows(tmp[:, :, :], node_rows(sums[1], D))
        with nc.Block() as block:
            @block.vector
            def _(dve):
                link(dve, dve.tensor_tensor(cat[:, :, 0:D], tmp[:, :, :], per_node(degree), ALU.mult))
                link(dve, dve.tensor_copy(cat[:, :, D:2 * D], h[:, :, :]))
        transpose_nodes(cat, 2 * D, hT[:, :])
        with nc.Block() as block:
            pe0, vec0 = at(s_pe), at(s_vec)
            cat_nodes = hT[:, :].rearrange("f (p t) -> f t p", t=NT)
            starts = list(range(0, NT, 8))

            @block.tensor
            def _(pe):
                for n, t0 in enumerate(starts):
                    if n >= 2:
                        pe.wait_ge(s_vec, vec0 + n - 1)
                    for t in range(t0, min(t0 + 8, NT)):
                        last = pe.matmul(banks[n % 2][:, (t - t0) * D:(t - t0 + 1) * D], cat_nodes[:, t, :],
                                         wv_sb[:, :], start=True, stop=True)
                    bump(s_pe, last)

            @block.vector
            def _(dve):
                for n, t0 in enumerate(starts):
                    dve.wait_ge(s_pe, pe0 + n + 1)
                    k = min(8, NT - t0)
                    bump(s_vec, dve.tensor_tensor(
                        tmp[:, t0:t0 + k, :], banks[n % 2][:, 0:k * D].rearrange("p (t f) -> p t f", f=D),
                        bv_sb[:, :].rearrange("p (o f) -> p o f", o=1).to_broadcast([P, k, D]), ALU.add))
                dve.wait_ge(s_vec, at(s_vec))
                link(dve, dve.scalar_tensor_tensor(x[:, :, :], tmp[:, :, :], 0.0, x[:, :, :], ALU.max, ALU.add))

        load_first_counts()
        layernorm_relu()
        add_neighbours(x[:, :, :], h_rows[2], sums[2])
        with nc.Block() as block:
            @block.sync
            def _(sp):
                bump(s_store, sp.dma_start(out.rearrange("(p t) f -> p t f", t=NT), x[:, :, :]), 16)
                sp.wait_ge(s_store, at(s_store))


def kernel(**inputs):
    import concourse.bacc as bacc
    from concourse.bass_utils import run_bass_kernel_spmd

    arrays = lay_out(inputs)
    nc = bacc.Bacc("TRN2", target_bir_lowering=False, num_devices=1)
    args = [nc.dram_tensor(name, a.shape, mybir.dt.from_np(a.dtype), kind="ExternalInput").ap()
            for name, a in arrays.items()]
    out = nc.dram_tensor("out", (NPAD, D), F32, kind="ExternalOutput").ap()
    gnn_layers(nc, *args, out)
    r = run_bass_kernel_spmd(nc, [arrays], core_ids=[0])
    return r.results[0]["out"][0:N]


def lay_out(inputs):
    a = {k: np.ascontiguousarray(v) for k, v in inputs.items()}
    pad = T * P - E

    def edges(v, fill=0):
        return np.concatenate([v, np.full((pad, *v.shape[1:]), fill, v.dtype)])

    dst = edges(a["dst"].astype(np.int32), NO_NODE)
    arrays = {
        "x_in": np.concatenate([a["x"], np.zeros((NPAD - N, D), np.float32)]),
        "src_c": edges(a["src"].astype(np.int32)).reshape(T, P).T,
        "dst_c": dst.reshape(T, P).T,
        "dst_r": dst.reshape(C, EC),
        "ea32_t": edges(a["edge_attr_32"]).T,
        "ea64_c": edges(a["edge_attr_64"]).reshape(C, G, P, D).transpose(0, 2, 1, 3),
        "beta": a["L0_gnn_beta"], "eps": a["L1_gnn_eps"],
        "w1": a["L1_gnn_W1"], "b1": a["L1_gnn_b1"], "gamma1": a["L1_gnn_gamma1"], "beta1": a["L1_gnn_beta1"],
        "w2": a["L1_gnn_W2"], "b2": a["L1_gnn_b2"], "gamma2": a["L1_gnn_gamma2"], "beta2": a["L1_gnn_beta2"],
        "w_e": a["L2_gnn_W_e"], "b_e": a["L2_gnn_b_e"], "w_v": a["L2_gnn_W_v"], "b_v": a["L2_gnn_b_v"],
    }
    return {k: np.ascontiguousarray(v) for k, v in arrays.items()}
```
